# Optimizing a Trainium2 kernel written in Bass

```python
import numpy as np
import jax
import jax.numpy as jnp

def _softmax(x, axis=-1):
    return jax.nn.softmax(x, axis=axis)

def _gelu(x):
    return jax.nn.gelu(x, approximate=True)

def _silu(x):
    return jax.nn.silu(x)

def _sigmoid(x):
    return jax.nn.sigmoid(x)

def _layernorm(x, axis=-1, eps=1e-05):
    m = jnp.mean(x, axis=axis, keepdims=True)
    v = jnp.var(x, axis=axis, keepdims=True)
    return (x - m) / jnp.sqrt(v + eps)

def _scatter_add(tgt, idx, src, axis=0):
    return tgt.at[idx].add(src)

def _segment_sum(src, seg, n):
    return jax.ops.segment_sum(src, seg, n)
kernel_name = 'mk_pixart_seq_d4_seqx_r8_9d4382'

def setup_inputs(seed: int=0):
    np.random.seed(seed)
    _w = jnp.asarray

    def _rec_inputs():
        import jax
        import jax.numpy as jnp
        _rk = jax.random.key(seed)
        x = -0.0003929 + 0.9999 * jax.random.normal(jax.random.fold_in(_rk, 1), (16, 56, 128), jnp.float32)
        _lenS = 56 - jax.random.randint(jax.random.fold_in(_rk, 7), (16,), 0, max(1, 56 // 4) + 1, jnp.int32)
        _lenS2 = 1500 - jax.random.randint(jax.random.fold_in(_rk, 8), (16,), 0, max(1, 1500 // 4) + 1, jnp.int32)
        cond_1024 = 0.00782532 + 1.00527 * jax.random.normal(jax.random.fold_in(_rk, 11), (16, 128), jnp.float32)
        _ctx_1024P = jax.random.normal(jax.random.fold_in(_rk, 12), (16, 16, 128), jnp.float32)
        _ctx_1024c = jax.random.dirichlet(jax.random.fold_in(_rk, 512), 0.3 * jnp.ones((16,), jnp.float32), (16, 1500))
        _ctx_1024t = jnp.einsum('bsk,bkd->bsd', _ctx_1024c, _ctx_1024P)
        _ctx_1024t = _ctx_1024t * jax.lax.rsqrt(jnp.mean(jnp.square(_ctx_1024t)) + 1e-12) * 0.953939
        ctx_1024 = -0.000761806 + 0.999296 * (_ctx_1024t + 0.3 * jax.random.normal(jax.random.fold_in(_rk, 612), (16, 1500, 128), jnp.float32))
        return (x, cond_1024, ctx_1024)
    x, cond_1024, ctx_1024 = _rec_inputs()

    def _L0_xcond_setup():
        import jax, jax.numpy as jnp
        import numpy as np
        H = 128
        RH = 2 * H
        E = 3
        B, T, P = (8, 256, 64)
        LN_EPS = 1e-05

        def _layer_norm(x, gamma, beta):
            mu = jnp.mean(x, axis=-1, keepdims=True)
            var = jnp.mean(jnp.square(x - mu), axis=-1, keepdims=True)
            return (x - mu) * jax.lax.rsqrt(var + LN_EPS) * gamma + beta
        key = jax.random.key(seed)
        ks = jax.random.split(key, 24)
        s = lambda fan_in: 1.0 / np.sqrt(fan_in)
        inp = {'mix_hidden_states': jax.random.normal(ks[0], (B, T, H), jnp.float32), 'global_anchor': jax.random.normal(ks[1], (B, H), jnp.float32), 'prototype_bank': jax.random.normal(ks[2], (B, P, H), jnp.float32), 'ln_gamma': jnp.ones((H,), jnp.float32), 'ln_beta': jnp.zeros((H,), jnp.float32), 'Wq': jax.random.normal(ks[3], (H, H), jnp.float32) * s(H), 'Wk': jax.random.normal(ks[4], (H, H), jnp.float32) * s(H), 'Wv': jax.random.normal(ks[5], (H, H), jnp.float32) * s(H), 'router_W': jax.random.normal(ks[6], (3 * H, E), jnp.float32) * s(3 * H), 'router_b': jnp.zeros((E,), jnp.float32), 'e_w1': jax.random.normal(ks[7], (E, 3 * H, RH), jnp.float32) * s(3 * H), 'e_b1': jnp.zeros((E, RH), jnp.float32), 'e_w2': jax.random.normal(ks[8], (E, RH, H), jnp.float32) * s(RH), 'e_b2': jnp.zeros((E, H), jnp.float32), 'gate_w1': jax.random.normal(ks[9], (3 * H, H), jnp.float32) * s(3 * H), 'gate_b1': jnp.zeros((H,), jnp.float32), 'gate_w2': jax.random.normal(ks[10], (H, H), jnp.float32) * s(H), 'gate_b2': jnp.zeros((H,), jnp.float32), 'out_w': jax.random.normal(ks[11], (H, H), jnp.float32) * s(H), 'out_b': jnp.zeros((H,), jnp.float32)}
        return inp
    _L0_xcond_all = _L0_xcond_setup()
    _L0_xcond_in = {k: v for k, v in _L0_xcond_all.items() if k in ('ln_gamma', 'ln_beta', 'Wq', 'Wk', 'Wv', 'router_W', 'router_b', 'e_w1', 'e_b1', 'e_w2', 'e_b2', 'gate_w1', 'gate_b1', 'gate_w2', 'gate_b2', 'out_w', 'out_b')}
    del _L0_xcond_all

    def _L1_xcond_setup():
        import jax, jax.numpy as jnp
        import numpy as np
        EPS = 1e-05

        def _ada_ln(x, c, W_ss, b_ss):
            mu = jnp.mean(x, axis=-1, keepdims=True)
            var = jnp.mean((x - mu) ** 2, axis=-1, keepdims=True)
            h = (x - mu) / jnp.sqrt(var + EPS)
            ss = jax.nn.silu(c) @ W_ss + b_ss
            scale, bias = jnp.split(ss, 2, axis=-1)
            return (1.0 + scale)[:, None, :] * h + bias[:, None, :]
        key = jax.random.key(seed)
        ks = jax.random.split(key, 12)
        B, Lq, Lkv, H = (8, 256, 64, 128)
        s = 0.02
        return {'x_q': jax.random.normal(ks[0], (B, Lq, H), jnp.float32), 'x_kv': jax.random.normal(ks[1], (B, Lkv, H), jnp.float32), 't_vec': jax.random.normal(ks[2], (B, H), jnp.float32), 'Wq': jax.random.normal(ks[3], (H, H), jnp.float32) * s, 'bq': jnp.zeros((H,), jnp.float32), 'Wkv': jax.random.normal(ks[4], (H, 2 * H), jnp.float32) * s, 'bkv': jnp.zeros((2 * H,), jnp.float32), 'Wp': jax.random.normal(ks[5], (H, H), jnp.float32) * s, 'bp': jnp.zeros((H,), jnp.float32), 'Wss_q': jax.random.normal(ks[6], (H, 2 * H), jnp.float32) * s, 'bss_q': jnp.zeros((2 * H,), jnp.float32), 'Wss_kv': jax.random.normal(ks[7], (H, 2 * H), jnp.float32) * s, 'bss_kv': jnp.zeros((2 * H,), jnp.float32)}
    _L1_xcond_all = _L1_xcond_setup()
    _L1_xcond_in = {k: v for k, v in _L1_xcond_all.items() if k in ('Wq', 'bq', 'Wkv', 'bkv', 'Wp', 'bp', 'Wss_q', 'bss_q', 'Wss_kv', 'bss_kv')}
    del _L1_xcond_all

    def _L2_xcond_setup():
        import jax, jax.numpy as jnp
        import numpy as np
        LN_EPS = 1e-06

        def _ln(x):
            mu = jnp.mean(x, axis=-1, keepdims=True)
            var = jnp.var(x, axis=-1, keepdims=True)
            return (x - mu) * jax.lax.rsqrt(var + LN_EPS)
        key = jax.random.key(seed)
        H, NH = (128, 16)
        B, N, S = (4, 128, 77)
        MLP = int(H * 4.0)
        ks = jax.random.split(key, 20)
        s = 1.0 / np.sqrt(H)
        return {'x': jax.random.normal(ks[0], (B, N, H), jnp.float32), 'c': jax.random.normal(ks[1], (B, H), jnp.float32), 'context': jax.random.normal(ks[2], (B, S, H), jnp.float32), 'W_mod': jax.random.normal(ks[3], (H, 6 * H), jnp.float32) * s, 'b_mod': jnp.zeros((6 * H,), jnp.float32), 'W_qkv': jax.random.normal(ks[4], (H, 3 * H), jnp.float32) * s, 'b_qkv': jnp.zeros((3 * H,), jnp.float32), 'W_proj': jax.random.normal(ks[5], (H, H), jnp.float32) * s, 'b_proj': jnp.zeros((H,), jnp.float32), 'W_qc': jax.random.normal(ks[6], (H, H), jnp.float32) * s, 'b_qc': jnp.zeros((H,), jnp.float32), 'W_kvc': jax.random.normal(ks[7], (H, 2 * H), jnp.float32) * s, 'b_kvc': jnp.zeros((2 * H,), jnp.float32), 'W_cproj': jax.random.normal(ks[8], (H, H), jnp.float32) * s, 'b_cproj': jnp.zeros((H,), jnp.float32), 'W_mlp1': jax.random.normal(ks[9], (H, MLP), jnp.float32) * s, 'b_mlp1': jnp.zeros((MLP,), jnp.float32), 'W_mlp2': jax.random.normal(ks[10], (MLP, H), jnp.float32) * (1.0 / np.sqrt(MLP)), 'b_mlp2': jnp.zeros((H,), jnp.float32)}
    _L2_xcond_all = _L2_xcond_setup()
    _L2_xcond_in = {k: v for k, v in _L2_xcond_all.items() if k in ('W_mod', 'b_mod', 'W_qkv', 'b_qkv', 'W_proj', 'b_proj', 'W_qc', 'b_qc', 'W_kvc', 'b_kvc', 'W_cproj', 'b_cproj', 'W_mlp1', 'b_mlp1', 'W_mlp2', 'b_mlp2')}
    del _L2_xcond_all

    def _L3_xcond_setup():
        import jax, jax.numpy as jnp
        import numpy as np
        D = 128
        H = 16
        DH = D // H
        DFF = 512
        B = 2
        L = 256
        EPS = 1e-05

        def layer_norm(x, g, b):
            mu = jnp.mean(x, axis=-1, keepdims=True)
            var = jnp.mean(jnp.square(x - mu), axis=-1, keepdims=True)
            return (x - mu) * jax.lax.rsqrt(var + EPS) * g + b

        def ada_ln(x, t_emb, ln_g, ln_b, aff_w, aff_b):
            normed = layer_norm(x, ln_g, ln_b)
            affine = t_emb @ aff_w + aff_b
            gamma, beta = jnp.split(affine, 2, axis=-1)
            return gamma[:, None, :] * normed + beta[:, None, :]

        def mha(q_in, k_in, v_in, qw, qb, kw, kb, vw, vb, ow, ob):
            Bq, Lq, _ = q_in.shape
            Lk = k_in.shape[1]
            Q = (q_in @ qw + qb).reshape(Bq, Lq, H, DH)
            K = (k_in @ kw + kb).reshape(Bq, Lk, H, DH)
            V = (v_in @ vw + vb).reshape(Bq, Lk, H, DH)
            scores = jnp.einsum('bqhd,bkhd->bhqk', Q, K) / np.sqrt(DH).astype(np.float32)
            attn = jax.nn.softmax(scores, axis=-1)
            out = jnp.einsum('bhqk,bkhd->bqhd', attn, V).reshape(Bq, Lq, D)
            return out @ ow + ob
        key = jax.random.key(seed)
        ks = jax.random.split(key, 32)
        s = lambda k, shape, scale=0.02: jax.random.normal(k, shape, dtype=jnp.float32) * scale
        inp = {'x': jax.random.normal(ks[0], (B, L, D), dtype=jnp.float32), 'u': jax.random.normal(ks[1], (B, L, D), dtype=jnp.float32), 't_emb': jax.random.normal(ks[2], (B, D), dtype=jnp.float32), 'ln1_g': jnp.ones((D,), jnp.float32), 'ln1_b': jnp.zeros((D,), jnp.float32), 'aff1_w': s(ks[3], (D, 2 * D)), 'aff1_b': jnp.zeros((2 * D,), jnp.float32), 'ln2_g': jnp.ones((D,), jnp.float32), 'ln2_b': jnp.zeros((D,), jnp.float32), 'aff2_w': s(ks[4], (D, 2 * D)), 'aff2_b': jnp.zeros((2 * D,), jnp.float32), 'sa_qw': s(ks[5], (D, D)), 'sa_qb': jnp.zeros((D,), jnp.float32), 'sa_kw': s(ks[6], (D, D)), 'sa_kb': jnp.zeros((D,), jnp.float32), 'sa_vw': s(ks[7], (D, D)), 'sa_vb': jnp.zeros((D,), jnp.float32), 'sa_ow': s(ks[8], (D, D)), 'sa_ob': jnp.zeros((D,), jnp.float32), 'ca_qw': s(ks[9], (D, D)), 'ca_qb': jnp.zeros((D,), jnp.float32), 'ca_kw': s(ks[10], (D, D)), 'ca_kb': jnp.zeros((D,), jnp.float32), 'ca_vw': s(ks[11], (D, D)), 'ca_vb': jnp.zeros((D,), jnp.float32), 'ca_ow': s(ks[12], (D, D)), 'ca_ob': jnp.zeros((D,), jnp.float32), 'ffn_w1': s(ks[13], (D, DFF)), 'ffn_b1': jnp.zeros((DFF,), jnp.float32), 'ffn_w2': s(ks[14], (DFF, D)), 'ffn_b2': jnp.zeros((D,), jnp.float32)}
        return inp
    _L3_xcond_all = _L3_xcond_setup()
    _L3_xcond_in = {k: v for k, v in _L3_xcond_all.items() if k in ('ln1_g', 'ln1_b', 'aff1_w', 'aff1_b', 'ln2_g', 'ln2_b', 'aff2_w', 'aff2_b', 'sa_qw', 'sa_qb', 'sa_kw', 'sa_kb', 'sa_vw', 'sa_vb', 'sa_ow', 'sa_ob', 'ca_qw', 'ca_qb', 'ca_kw', 'ca_kb', 'ca_vw', 'ca_vb', 'ca_ow', 'ca_ob', 'ffn_w1', 'ffn_b1', 'ffn_w2', 'ffn_b2')}
    del _L3_xcond_all
    return {'x': x, 'cond_1024': cond_1024, 'ctx_1024': ctx_1024, 'L0_xcond_ln_gamma': _L0_xcond_in['ln_gamma'], 'L0_xcond_ln_beta': _L0_xcond_in['ln_beta'], 'L0_xcond_Wq': _L0_xcond_in['Wq'], 'L0_xcond_Wk': _L0_xcond_in['Wk'], 'L0_xcond_Wv': _L0_xcond_in['Wv'], 'L0_xcond_router_W': _L0_xcond_in['router_W'], 'L0_xcond_router_b': _L0_xcond_in['router_b'], 'L0_xcond_e_w1': _L0_xcond_in['e_w1'], 'L0_xcond_e_b1': _L0_xcond_in['e_b1'], 'L0_xcond_e_w2': _L0_xcond_in['e_w2'], 'L0_xcond_e_b2': _L0_xcond_in['e_b2'], 'L0_xcond_gate_w1': _L0_xcond_in['gate_w1'], 'L0_xcond_gate_b1': _L0_xcond_in['gate_b1'], 'L0_xcond_gate_w2': _L0_xcond_in['gate_w2'], 'L0_xcond_gate_b2': _L0_xcond_in['gate_b2'], 'L0_xcond_out_w': _L0_xcond_in['out_w'], 'L0_xcond_out_b': _L0_xcond_in['out_b'], 'L1_xcond_Wq': _L1_xcond_in['Wq'], 'L1_xcond_bq': _L1_xcond_in['bq'], 'L1_xcond_Wkv': _L1_xcond_in['Wkv'], 'L1_xcond_bkv': _L1_xcond_in['bkv'], 'L1_xcond_Wp': _L1_xcond_in['Wp'], 'L1_xcond_bp': _L1_xcond_in['bp'], 'L1_xcond_Wss_q': _L1_xcond_in['Wss_q'], 'L1_xcond_bss_q': _L1_xcond_in['bss_q'], 'L1_xcond_Wss_kv': _L1_xcond_in['Wss_kv'], 'L1_xcond_bss_kv': _L1_xcond_in['bss_kv'], 'L2_xcond_W_mod': _L2_xcond_in['W_mod'], 'L2_xcond_b_mod': _L2_xcond_in['b_mod'], 'L2_xcond_W_qkv': _L2_xcond_in['W_qkv'], 'L2_xcond_b_qkv': _L2_xcond_in['b_qkv'], 'L2_xcond_W_proj': _L2_xcond_in['W_proj'], 'L2_xcond_b_proj': _L2_xcond_in['b_proj'], 'L2_xcond_W_qc': _L2_xcond_in['W_qc'], 'L2_xcond_b_qc': _L2_xcond_in['b_qc'], 'L2_xcond_W_kvc': _L2_xcond_in['W_kvc'], 'L2_xcond_b_kvc': _L2_xcond_in['b_kvc'], 'L2_xcond_W_cproj': _L2_xcond_in['W_cproj'], 'L2_xcond_b_cproj': _L2_xcond_in['b_cproj'], 'L2_xcond_W_mlp1': _L2_xcond_in['W_mlp1'], 'L2_xcond_b_mlp1': _L2_xcond_in['b_mlp1'], 'L2_xcond_W_mlp2': _L2_xcond_in['W_mlp2'], 'L2_xcond_b_mlp2': _L2_xcond_in['b_mlp2'], 'L3_xcond_ln1_g': _L3_xcond_in['ln1_g'], 'L3_xcond_ln1_b': _L3_xcond_in['ln1_b'], 'L3_xcond_aff1_w': _L3_xcond_in['aff1_w'], 'L3_xcond_aff1_b': _L3_xcond_in['aff1_b'], 'L3_xcond_ln2_g': _L3_xcond_in['ln2_g'], 'L3_xcond_ln2_b': _L3_xcond_in['ln2_b'], 'L3_xcond_aff2_w': _L3_xcond_in['aff2_w'], 'L3_xcond_aff2_b': _L3_xcond_in['aff2_b'], 'L3_xcond_sa_qw': _L3_xcond_in['sa_qw'], 'L3_xcond_sa_qb': _L3_xcond_in['sa_qb'], 'L3_xcond_sa_kw': _L3_xcond_in['sa_kw'], 'L3_xcond_sa_kb': _L3_xcond_in['sa_kb'], 'L3_xcond_sa_vw': _L3_xcond_in['sa_vw'], 'L3_xcond_sa_vb': _L3_xcond_in['sa_vb'], 'L3_xcond_sa_ow': _L3_xcond_in['sa_ow'], 'L3_xcond_sa_ob': _L3_xcond_in['sa_ob'], 'L3_xcond_ca_qw': _L3_xcond_in['ca_qw'], 'L3_xcond_ca_qb': _L3_xcond_in['ca_qb'], 'L3_xcond_ca_kw': _L3_xcond_in['ca_kw'], 'L3_xcond_ca_kb': _L3_xcond_in['ca_kb'], 'L3_xcond_ca_vw': _L3_xcond_in['ca_vw'], 'L3_xcond_ca_vb': _L3_xcond_in['ca_vb'], 'L3_xcond_ca_ow': _L3_xcond_in['ca_ow'], 'L3_xcond_ca_ob': _L3_xcond_in['ca_ob'], 'L3_xcond_ffn_w1': _L3_xcond_in['ffn_w1'], 'L3_xcond_ffn_b1': _L3_xcond_in['ffn_b1'], 'L3_xcond_ffn_w2': _L3_xcond_in['ffn_w2'], 'L3_xcond_ffn_b2': _L3_xcond_in['ffn_b2']}

def reference(x, cond_1024, ctx_1024, L0_xcond_ln_gamma, L0_xcond_ln_beta, L0_xcond_Wq, L0_xcond_Wk, L0_xcond_Wv, L0_xcond_router_W, L0_xcond_router_b, L0_xcond_e_w1, L0_xcond_e_b1, L0_xcond_e_w2, L0_xcond_e_b2, L0_xcond_gate_w1, L0_xcond_gate_b1, L0_xcond_gate_w2, L0_xcond_gate_b2, L0_xcond_out_w, L0_xcond_out_b, L1_xcond_Wq, L1_xcond_bq, L1_xcond_Wkv, L1_xcond_bkv, L1_xcond_Wp, L1_xcond_bp, L1_xcond_Wss_q, L1_xcond_bss_q, L1_xcond_Wss_kv, L1_xcond_bss_kv, L2_xcond_W_mod, L2_xcond_b_mod, L2_xcond_W_qkv, L2_xcond_b_qkv, L2_xcond_W_proj, L2_xcond_b_proj, L2_xcond_W_qc, L2_xcond_b_qc, L2_xcond_W_kvc, L2_xcond_b_kvc, L2_xcond_W_cproj, L2_xcond_b_cproj, L2_xcond_W_mlp1, L2_xcond_b_mlp1, L2_xcond_W_mlp2, L2_xcond_b_mlp2, L3_xcond_ln1_g, L3_xcond_ln1_b, L3_xcond_aff1_w, L3_xcond_aff1_b, L3_xcond_ln2_g, L3_xcond_ln2_b, L3_xcond_aff2_w, L3_xcond_aff2_b, L3_xcond_sa_qw, L3_xcond_sa_qb, L3_xcond_sa_kw, L3_xcond_sa_kb, L3_xcond_sa_vw, L3_xcond_sa_vb, L3_xcond_sa_ow, L3_xcond_sa_ob, L3_xcond_ca_qw, L3_xcond_ca_qb, L3_xcond_ca_kw, L3_xcond_ca_kb, L3_xcond_ca_vw, L3_xcond_ca_vb, L3_xcond_ca_ow, L3_xcond_ca_ob, L3_xcond_ffn_w1, L3_xcond_ffn_b1, L3_xcond_ffn_w2, L3_xcond_ffn_b2):
    import jax
    import jax.numpy as jnp

    def _L0_xcond_ref(mix_hidden_states, global_anchor, prototype_bank, ln_gamma, ln_beta, Wq, Wk, Wv, router_W, router_b, e_w1, e_b1, e_w2, e_b2, gate_w1, gate_b1, gate_w2, gate_b2, out_w, out_b):
        import jax, jax.numpy as jnp
        import numpy as np
        H = 128
        RH = 2 * H
        E = 3
        B, T, P = (8, 256, 64)
        LN_EPS = 1e-05

        def _layer_norm(x, gamma, beta):
            mu = jnp.mean(x, axis=-1, keepdims=True)
            var = jnp.mean(jnp.square(x - mu), axis=-1, keepdims=True)
            return (x - mu) * jax.lax.rsqrt(var + LN_EPS) * gamma + beta
        x = mix_hidden_states
        nx = _layer_norm(x, ln_gamma, ln_beta)
        q = nx @ Wq
        k = prototype_bank @ Wk
        v = prototype_bank @ Wv
        scores = jnp.einsum('bth,bph->btp', q, k) * H ** (-0.5)
        weights = jax.nn.softmax(scores, axis=-1)
        evidence = jnp.einsum('btp,bph->bth', weights, v)
        anchor = jnp.broadcast_to(global_anchor[:, None, :], nx.shape)
        combined = jnp.concatenate([nx, evidence, anchor], axis=-1)
        router_logits = combined @ router_W + router_b
        router_probs = jax.nn.softmax(router_logits, axis=-1)
        h = jax.nn.silu(jnp.einsum('btc,ecr->bter', combined, e_w1) + e_b1)
        expert_out = jnp.einsum('bter,erh->bteh', h, e_w2) + e_b2
        routed = jnp.sum(expert_out * router_probs[..., None], axis=-2)
        g = jax.nn.sigmoid(jax.nn.silu(combined @ gate_w1 + gate_b1) @ gate_w2 + gate_b2)
        refined_delta = g * (routed @ out_w + out_b)
        return x + refined_delta

    def _L1_xcond_ref(x_q, x_kv, t_vec, Wq, bq, Wkv, bkv, Wp, bp, Wss_q, bss_q, Wss_kv, bss_kv):
        import jax, jax.numpy as jnp
        import numpy as np
        EPS = 1e-05

        def _ada_ln(x, c, W_ss, b_ss):
            mu = jnp.mean(x, axis=-1, keepdims=True)
            var = jnp.mean((x - mu) ** 2, axis=-1, keepdims=True)
            h = (x - mu) / jnp.sqrt(var + EPS)
            ss = jax.nn.silu(c) @ W_ss + b_ss
            scale, bias = jnp.split(ss, 2, axis=-1)
            return (1.0 + scale)[:, None, :] * h + bias[:, None, :]
        B, Lq, H = x_q.shape
        Lkv = x_kv.shape[1]
        nh = 16
        dh = H // nh
        xq = _ada_ln(x_q, t_vec, Wss_q, bss_q)
        xkv = _ada_ln(x_kv, t_vec, Wss_kv, bss_kv)
        q = (xq @ Wq + bq).reshape(B, Lq, nh, dh)
        kv = (xkv @ Wkv + bkv).reshape(B, Lkv, 2, nh, dh)
        k = kv[:, :, 0]
        v = kv[:, :, 1]
        scores = jnp.einsum('bqhd,bkhd->bhqk', q, k) / jnp.sqrt(jnp.float32(dh))
        attn = jax.nn.softmax(scores, axis=-1)
        out = jnp.einsum('bhqk,bkhd->bqhd', attn, v).reshape(B, Lq, H)
        return x_q + (out @ Wp + bp)

    def _L2_xcond_ref(x, c, context, W_mod, b_mod, W_qkv, b_qkv, W_proj, b_proj, W_qc, b_qc, W_kvc, b_kvc, W_cproj, b_cproj, W_mlp1, b_mlp1, W_mlp2, b_mlp2):
        import jax, jax.numpy as jnp
        import numpy as np
        LN_EPS = 1e-06

        def _ln(x):
            mu = jnp.mean(x, axis=-1, keepdims=True)
            var = jnp.var(x, axis=-1, keepdims=True)
            return (x - mu) * jax.lax.rsqrt(var + LN_EPS)
        B, N, H = x.shape
        NH = 16
        hd = H // NH
        scale = hd ** (-0.5)
        c_proj = jax.nn.silu(c) @ W_mod + b_mod
        shift_a, scale_a, gate_a, shift_m, scale_m, gate_m = jnp.split(c_proj, 6, axis=-1)

        def modulate(t, shift, sc):
            return t * (1 + sc[:, None]) + shift[:, None]
        x_norm = modulate(_ln(x), shift_a, scale_a)
        qkv = x_norm @ W_qkv + b_qkv
        q, k, v = jnp.split(qkv, 3, axis=-1)
        q = q.reshape(B, N, NH, hd).transpose(0, 2, 1, 3)
        k = k.reshape(B, N, NH, hd).transpose(0, 2, 1, 3)
        v = v.reshape(B, N, NH, hd).transpose(0, 2, 1, 3)
        attn_w = jax.nn.softmax(jnp.einsum('bhqd,bhkd->bhqk', q, k) * scale, axis=-1)
        attn_out = jnp.einsum('bhqk,bhkd->bhqd', attn_w, v)
        attn_out = attn_out.transpose(0, 2, 1, 3).reshape(B, N, H)
        attn_out = attn_out @ W_proj + b_proj
        x = x + gate_a[:, None] * attn_out
        S = context.shape[1]
        q_c = _ln(x) @ W_qc + b_qc
        kv_c = _ln(context) @ W_kvc + b_kvc
        k_c, v_c = jnp.split(kv_c, 2, axis=-1)
        q_c = q_c.reshape(B, N, NH, hd).transpose(0, 2, 1, 3)
        k_c = k_c.reshape(B, S, NH, hd).transpose(0, 2, 1, 3)
        v_c = v_c.reshape(B, S, NH, hd).transpose(0, 2, 1, 3)
        c_attn_w = jax.nn.softmax(jnp.einsum('bhqd,bhsd->bhqs', q_c, k_c) * scale, axis=-1)
        c_attn_out = jnp.einsum('bhqs,bhsd->bhqd', c_attn_w, v_c)
        c_attn_out = c_attn_out.transpose(0, 2, 1, 3).reshape(B, N, H)
        c_attn_out = c_attn_out @ W_cproj + b_cproj
        x = x + c_attn_out
        x_norm2 = modulate(_ln(x), shift_m, scale_m)
        h = jax.nn.gelu(x_norm2 @ W_mlp1 + b_mlp1)
        h = h @ W_mlp2 + b_mlp2
        x = x + gate_m[:, None] * h
        return x

    def _L3_xcond_ref(x, u, t_emb, ln1_g, ln1_b, aff1_w, aff1_b, ln2_g, ln2_b, aff2_w, aff2_b, sa_qw, sa_qb, sa_kw, sa_kb, sa_vw, sa_vb, sa_ow, sa_ob, ca_qw, ca_qb, ca_kw, ca_kb, ca_vw, ca_vb, ca_ow, ca_ob, ffn_w1, ffn_b1, ffn_w2, ffn_b2):
        import jax, jax.numpy as jnp
        import numpy as np
        D = 128
        H = 16
        DH = D // H
        DFF = 512
        B = 2
        L = 256
        EPS = 1e-05

        def layer_norm(x, g, b):
            mu = jnp.mean(x, axis=-1, keepdims=True)
            var = jnp.mean(jnp.square(x - mu), axis=-1, keepdims=True)
            return (x - mu) * jax.lax.rsqrt(var + EPS) * g + b

        def ada_ln(x, t_emb, ln_g, ln_b, aff_w, aff_b):
            normed = layer_norm(x, ln_g, ln_b)
            affine = t_emb @ aff_w + aff_b
            gamma, beta = jnp.split(affine, 2, axis=-1)
            return gamma[:, None, :] * normed + beta[:, None, :]

        def mha(q_in, k_in, v_in, qw, qb, kw, kb, vw, vb, ow, ob):
            Bq, Lq, _ = q_in.shape
            Lk = k_in.shape[1]
            Q = (q_in @ qw + qb).reshape(Bq, Lq, H, DH)
            K = (k_in @ kw + kb).reshape(Bq, Lk, H, DH)
            V = (v_in @ vw + vb).reshape(Bq, Lk, H, DH)
            scores = jnp.einsum('bqhd,bkhd->bhqk', Q, K) / np.sqrt(DH).astype(np.float32)
            attn = jax.nn.softmax(scores, axis=-1)
            out = jnp.einsum('bhqk,bkhd->bqhd', attn, V).reshape(Bq, Lq, D)
            return out @ ow + ob
        xn = ada_ln(x, t_emb, ln1_g, ln1_b, aff1_w, aff1_b)
        x = x + mha(xn, xn, xn, sa_qw, sa_qb, sa_kw, sa_kb, sa_vw, sa_vb, sa_ow, sa_ob)
        x = x + mha(x, u, u, ca_qw, ca_qb, ca_kw, ca_kb, ca_vw, ca_vb, ca_ow, ca_ob)
        xn = ada_ln(x, t_emb, ln2_g, ln2_b, aff2_w, aff2_b)
        h = jax.nn.gelu(xn @ ffn_w1 + ffn_b1, approximate=False)
        x = x + (h @ ffn_w2 + ffn_b2)
        return x
    x = _L0_xcond_ref(x, cond_1024, ctx_1024, L0_xcond_ln_gamma, L0_xcond_ln_beta, L0_xcond_Wq, L0_xcond_Wk, L0_xcond_Wv, L0_xcond_router_W, L0_xcond_router_b, L0_xcond_e_w1, L0_xcond_e_b1, L0_xcond_e_w2, L0_xcond_e_b2, L0_xcond_gate_w1, L0_xcond_gate_b1, L0_xcond_gate_w2, L0_xcond_gate_b2, L0_xcond_out_w, L0_xcond_out_b)
    x = _L1_xcond_ref(x, ctx_1024, cond_1024, L1_xcond_Wq, L1_xcond_bq, L1_xcond_Wkv, L1_xcond_bkv, L1_xcond_Wp, L1_xcond_bp, L1_xcond_Wss_q, L1_xcond_bss_q, L1_xcond_Wss_kv, L1_xcond_bss_kv)
    x = _L2_xcond_ref(x, cond_1024, ctx_1024, L2_xcond_W_mod, L2_xcond_b_mod, L2_xcond_W_qkv, L2_xcond_b_qkv, L2_xcond_W_proj, L2_xcond_b_proj, L2_xcond_W_qc, L2_xcond_b_qc, L2_xcond_W_kvc, L2_xcond_b_kvc, L2_xcond_W_cproj, L2_xcond_b_cproj, L2_xcond_W_mlp1, L2_xcond_b_mlp1, L2_xcond_W_mlp2, L2_xcond_b_mlp2)
    x = _L3_xcond_ref(x, ctx_1024, cond_1024, L3_xcond_ln1_g, L3_xcond_ln1_b, L3_xcond_aff1_w, L3_xcond_aff1_b, L3_xcond_ln2_g, L3_xcond_ln2_b, L3_xcond_aff2_w, L3_xcond_aff2_b, L3_xcond_sa_qw, L3_xcond_sa_qb, L3_xcond_sa_kw, L3_xcond_sa_kb, L3_xcond_sa_vw, L3_xcond_sa_vb, L3_xcond_sa_ow, L3_xcond_sa_ob, L3_xcond_ca_qw, L3_xcond_ca_qb, L3_xcond_ca_kw, L3_xcond_ca_kb, L3_xcond_ca_vw, L3_xcond_ca_vb, L3_xcond_ca_ow, L3_xcond_ca_ob, L3_xcond_ffn_w1, L3_xcond_ffn_b1, L3_xcond_ffn_w2, L3_xcond_ffn_b2)
    return x

_drawn_inputs = setup_inputs


def setup_inputs(seed=0):
    import zlib

    import numpy as np

    out = dict(_drawn_inputs(seed))
    spreads = {'L0_xcond_ln_gamma': (1.0, 0.551),
     'L0_xcond_ln_beta': (0.0, 0.639),
     'L0_xcond_router_b': (0.0, 0.8),
     'L0_xcond_e_b1': (0.0, 0.395),
     'L0_xcond_e_b2': (0.0, 0.1),
     'L0_xcond_gate_b1': (0.0, 0.8),
     'L0_xcond_gate_b2': (0.0, 0.8),
     'L0_xcond_out_b': (0.0, 0.1),
     'L1_xcond_bq': (0.0, 2.0),
     'L1_xcond_bkv': (0.0, 0.337),
     'L1_xcond_bp': (0.0, 0.1),
     'L1_xcond_bss_q': (0.0, 2.0),
     'L1_xcond_bss_kv': (0.0, 0.8),
     'L2_xcond_b_mod': (0.0, 0.1),
     'L2_xcond_b_qkv': (0.0, 0.1),
     'L2_xcond_b_proj': (0.0, 0.1),
     'L2_xcond_b_qc': (0.0, 0.573),
     'L2_xcond_b_kvc': (0.0, 0.1),
     'L2_xcond_b_cproj': (0.0, 0.1),
     'L2_xcond_b_mlp1': (0.0, 0.1),
     'L2_xcond_b_mlp2': (0.0, 0.1),
     'L3_xcond_ln1_g': (1.0, 0.6),
     'L3_xcond_ln1_b': (0.0, 0.8),
     'L3_xcond_aff1_b': (0.0, 0.8),
     'L3_xcond_ln2_g': (1.0, 0.6),
     'L3_xcond_ln2_b': (0.0, 0.8),
     'L3_xcond_aff2_b': (0.0, 0.8),
     'L3_xcond_sa_qb': (0.0, 0.8),
     'L3_xcond_sa_kb': (0.0, 2.0),
     'L3_xcond_sa_vb': (0.0, 0.46),
     'L3_xcond_sa_ob': (0.0, 0.1),
     'L3_xcond_ca_qb': (0.0, 2.0),
     'L3_xcond_ca_kb': (0.0, 2.0),
     'L3_xcond_ca_vb': (0.0, 0.526),
     'L3_xcond_ca_ob': (0.0, 0.1),
     'L3_xcond_ffn_b1': (0.0, 0.461),
     'L3_xcond_ffn_b2': (0.0, 0.1)}
    factors = {'L1_xcond_Wq': 8.0,
     'L1_xcond_Wss_q': 8.0,
     'L1_xcond_Wss_kv': 6.784,
     'L3_xcond_aff1_w': 5.953,
     'L3_xcond_aff2_w': 4.566,
     'L3_xcond_sa_qw': 8.0,
     'L3_xcond_sa_kw': 8.0,
     'L3_xcond_sa_vw': 5.463,
     'L3_xcond_sa_ow': 2.711,
     'L3_xcond_ca_qw': 8.0,
     'L3_xcond_ca_kw': 8.0,
     'L3_xcond_ca_vw': 2.953,
     'L3_xcond_ffn_w1': 4.165}
    for name, (base, spread) in spreads.items():
        noise = np.random.default_rng([zlib.crc32(name.encode()), seed]).standard_normal(out[name].shape)
        drawn = base * np.exp(spread * noise) if base else spread * noise
        out[name] = jnp.asarray(drawn.astype(out[name].dtype))
    for name, factor in factors.items():
        out[name] = (out[name] * factor).astype(out[name].dtype)
    return out
```

```python
from contextlib import ExitStack

import concourse.bass as bass
from concourse import mybir

F32 = mybir.dt.float32
F16 = mybir.dt.float16
ALU = mybir.AluOpType
ACT = mybir.ActivationFunctionType
AX = mybir.AxisListType

B, T, D = 16, 56, 128
S = 1500
C = 12
KC = S // C
NT = 3
TC = C // NT
TK = S // NT
NH, DH = 16, 8
HG = 4
NG = NH // HG
GW = HG * T
PW = 2 * T
NP = NH // 2
R = B * T
HR = R // 2
RT = R // PW
E = 3
DFF = 4 * D
ROWS = 99
UNITS = NP * NT
LOOPS = B // 2 - 1

SC_BANKS = ((0, 2), (2, 4))
MX_BANK = 4
PV_BANK = 6
MISC_BANK = 7

MISC = [("T", 0), ("T", 1), ("T", 2), ("K", 0), ("K", 1), ("K", 2), ("V", 0), ("V", 1), ("V", 2)]
SLOT_MISC = {0: (True, 8), 1: (False, 0), 2: (False, 1), 3: (False, 2), 4: (False, 3), 5: (False, 4),
             6: (False, 5), 7: (False, 6), 10: (False, 7)}
MAXES = [2, 3, 3, 3, 2, 2, 2, 2, 2, 3, 0, 0]
NORMS = [0, 2, 2, 2, 0, 0, 0, 2, 2, 2, 0, 0]
SHIFT_SLOT = 10
PIECES = ((0, 2 * TK), (2 * TK, S))
PIECE_OF = (0, 0, 1)
STACKED = 16 * 3 * NG

WEIGHTS = [
    "L0_xcond_Wq", "L0_xcond_Wk", "L0_xcond_Wv", "L0_xcond_gate_w1", "L0_xcond_gate_w2", "L0_xcond_out_w",
    "L0_xcond_router_W",
    "L1_xcond_Wq", "L1_xcond_Wkv", "L1_xcond_Wp", "L1_xcond_Wss_q", "L1_xcond_Wss_kv",
    "L2_xcond_W_mod", "L2_xcond_W_qkv", "L2_xcond_W_proj", "L2_xcond_W_qc", "L2_xcond_W_kvc", "L2_xcond_W_cproj",
    "L2_xcond_W_mlp1", "L2_xcond_W_mlp2",
    "L3_xcond_aff1_w", "L3_xcond_aff2_w", "L3_xcond_sa_qw", "L3_xcond_sa_kw", "L3_xcond_sa_vw", "L3_xcond_sa_ow",
    "L3_xcond_ca_qw", "L3_xcond_ca_kw", "L3_xcond_ca_vw", "L3_xcond_ca_ow", "L3_xcond_ffn_w1", "L3_xcond_ffn_w2",
]
VECTORS = [
    "L0_xcond_ln_gamma", "L0_xcond_ln_beta", "L0_xcond_gate_b1", "L0_xcond_gate_b2", "L0_xcond_out_b",
    "L0_xcond_e_b1", "L0_xcond_e_b2",
    "L1_xcond_bq", "L1_xcond_bkv", "L1_xcond_bp",
    "L2_xcond_b_qkv", "L2_xcond_b_proj", "L2_xcond_b_qc", "L2_xcond_b_kvc", "L2_xcond_b_cproj",
    "L2_xcond_b_mlp1", "L2_xcond_b_mlp2",
    "L3_xcond_ln1_g", "L3_xcond_ln1_b", "L3_xcond_ln2_g", "L3_xcond_ln2_b",
    "L3_xcond_sa_qb", "L3_xcond_sa_kb", "L3_xcond_sa_vb", "L3_xcond_sa_ob",
    "L3_xcond_ca_qb", "L3_xcond_ca_kb", "L3_xcond_ca_vb", "L3_xcond_ca_ob", "L3_xcond_ffn_b1", "L3_xcond_ffn_b2",
    "L1_xcond_bss_q", "L1_xcond_bss_kv", "L2_xcond_b_mod", "L3_xcond_aff1_b", "L3_xcond_aff2_b",
]
MODS = [("L1_xcond_Wss_q", 2), ("L1_xcond_Wss_kv", 2), ("L2_xcond_W_mod", 6), ("L3_xcond_aff1_w", 2), ("L3_xcond_aff2_w", 2)]
(Q_SCALE, Q_SHIFT, KV_SCALE, KV_SHIFT, SHIFT_A, SCALE_A, GATE_A, SHIFT_M, SCALE_M, GATE_M,
 GAMMA_1, BETA_1, GAMMA_2, BETA_2) = range(14)
NM = 14


def build(nc, x, cond, ctx, w, out, layers=4):
    with ExitStack() as stack:
        sems = {}

        def sem(name):
            if name not in sems:
                sems[name] = stack.enter_context(nc.semaphore(name))
            return sems[name]

        def sb(name, shape, dt=F32):
            return stack.enter_context(nc.sbuf_tensor(name, shape, dt))

        PS = stack.enter_context(nc.psum_tensor("PS", [128, 8, 512], F32))

        W = {}
        for name in WEIGHTS:
            rows, cols = w[name].shape
            W[name] = sb(name, [128, rows // 128, cols])
        w1 = sb("w1", [128, E, 3, 2 * D])
        w2 = sb("w2", [128, E, 2, D])
        place, nv = {}, 0
        for name in VECTORS:
            place[name] = nv
            n = 1
            for s in w[name].shape:
                n *= s
            nv += n // 128
        assert nv <= 128
        vrows = sb("vrows", [nv, 128])
        vec = sb("vec", [128, nv])
        router_b = sb("router_b", [128, E])

        def col(name, k=0):
            return vec[:, place[name] + k:place[name] + k + 1]

        half = sb("half", [128, 8])
        ident = sb("ident", [128, 128])
        ident16 = sb("ident16", [128, 128], F16)
        mean_w = sb("mean_w", [128, 128])
        ones32 = sb("ones32", [128, 32])
        mask = sb("mask", [128, HG])
        sel_mask = sb("sel_mask", [128, 2, HG, T])
        eps = sb("eps", [128, 2])
        wkT = sb("wkT", [128, D])
        cond_sb = sb("cond_sb", [B, D])
        condT = sb("condT", [128, B])
        silu_t = sb("silu_t", [128, B])
        siluT = sb("siluT", [128, B])
        mod = sb("mod", [128, NM, B])

        X = sb("X", [128, R])
        A = [sb(f"A{i}", [128, R]) for i in range(10)]
        CEN, SQ, STD, XH = A[0], A[1], A[2], A[3]
        OALL = sb("OALL", [128, R])

        cx = sb("cx", [KC, 2, C, D])
        cxT = sb("cxT", [128, S])
        xrows = cxT[0:PW, 0:RT * D].rearrange("p (k d) -> p k d", k=RT)
        mean_all = sb("mean_all", [KC, B, C])
        var_all = sb("var_all", [KC, B, C])
        std_all = sb("std_all", [KC, B, C])
        rstd_all = sb("rstd_all", [KC, 2, B, C])
        stats = sb("stats", [KC, C, 6])
        aggr = sb("aggr", [KC, C, 2])
        norm_b = sb("norm_b", [KC, 2, 2, C])
        mod_b = sb("mod_b", [128, 2, 2])

        k_hi = sb("k_hi", [128, S], F16)
        k_lo = sb("k_lo", [128, S], F16)
        k_st = sb("k_st", [128, 2, NG, S], F16)
        q_all = sb("q_all", [96, NG, B, GW], F16)
        q_st = sb("q_st", [128, 2, NG, GW], F16)
        q_mx = sb("q_mx", [96, 2, NG, GW], F16)
        v_sb = sb("v_sb", [KC, 2, C, D])
        mx = sb("mx", [PW, NP, NT])
        mneg = sb("mneg", [PW, NP])
        mrest = sb("mrest", [PW, 2, NP])
        msplit = sb("msplit", [PW, NP, 3], F16)
        sel = sb("sel", [128, 2, HG, T])
        osum = sb("osum", [128, 2, T])
        orec = sb("orec", [128, T])

        q_parts = sb("q_parts", [128, 4 * R])
        probs = q_parts[0:KC, 0:3 * R].rearrange("p (n r) -> p n r", n=3)
        qh_all = q_parts[:, 0:2 * R].bitcast(F16).rearrange("p (b h t) -> p b h t", b=B, h=HG)
        ql_all = q_parts[:, 2 * R:4 * R].bitcast(F16).rearrange("p (b h t) -> p b h t", b=B, h=HG)

        qk_b = sb("qk_b", [128, 2, T])
        p0 = k_st[0:T, :, :, :].rearrange("p a g s -> p a (g s)").bitcast(F32)[:, :, 0:S]
        pT0 = probs[0:KC, 0, 0:C * T]
        ev_rows = sb("ev_rows", [T, D])
        neg0 = sb("neg0", [T, 2])
        sum0 = sb("sum0", [T, 2])
        rec0 = sb("rec0", [T, 2])
        xn_b = sb("xn_b", [128, 2, T])
        kk_b = sb("kk_b", [128, 2, T])
        qm_b = A[9][:, 0:2 * GW].rearrange("p (a h t) -> p a h t", a=2, h=HG)
        vv_b = sb("vv_b", [T, 2, D])
        s_sh = A[7][0:PW, :].rearrange("p (a h t) -> p a h t", a=2, h=NP)
        s_mx = sb("s_mx", [PW, NP])
        s_sum = sb("s_sum", [PW, NP])
        s_rec = sb("s_rec", [PW, NP])
        pT_b = A[8][0:T, :]

        def ge(eng, name, value=1):
            if not (isinstance(value, int) and value <= 0):
                eng.wait_ge(sem(name), value)

        def batches(eng, first, both, last, peel=False):
            first((0, 0, 0))
            if peel:
                both((0, 0, 0), (1, 0, 1), True)
                both((1, 0, 1), (2, 1, 0), True)
            with eng.Fori(1 if peel else 0, LOOPS) as i:
                both((2 * i, i, 0), (2 * i + 1, i, 1), True)
                both((2 * i + 1, i, 1), (2 * i + 2, i + 1, 0), True)
            both((B - 2, B // 2 - 1, 0), (B - 1, B // 2 - 1, 1), False)
            last((B - 1, B // 2 - 1, 1))

        def pipeline(eng, first, body):
            def at(b, i=None):
                return (b, b // 2, b % 2) if i is None else (2 * i + b, i + b // 2, b % 2)

            first()
            for b in range(2):
                body(*[at(b + k) for k in range(4)])
            with eng.Fori(1, B // 2 - 2) as i:
                for b in range(2):
                    body(*[at(b + k, i) for k in range(4)])
            for b in range(B - 4, B):
                body(*[at(b + k) if b + k < B else None for k in range(4)])

        def ge_ahead(pe, *waits):
            values = [(name, v if isinstance(v, int) else pe.snap(v)) for name, v in waits]
            pe.wait_ge(sem("ident_done"), 1)
            for name, v in values:
                ge(pe, name, v)

        def rows_of(t, b):
            return t[:, bass.ds(b * T, T)]

        def pair(k):
            return PS[:, 2 * k:2 * k + 2, 0:HR]

        def halves(t):
            return t.rearrange("p (u r) -> p u r", u=2) if isinstance(t, bass.AP) else t[:, :].rearrange("p (u r) -> p u r", u=2)

        def by_batch(t):
            return t[:, :].rearrange("p (b t) -> p b t", b=B)

        def spread(k):
            return mod[:, k, :].unsqueeze(2).to_broadcast([128, B, T])

        block = stack.enter_context(nc.Block())

        def cross_of(layer):
            if layer == 1:
                return dict(n=0, norm=0, mod=True, kw=W["L1_xcond_Wkv"][:, 0, 0:D], vw=W["L1_xcond_Wkv"][:, 0, D:2 * D],
                            kb=col("L1_xcond_bkv", 0), vb=col("L1_xcond_bkv", 1),
                            ow=W["L1_xcond_Wp"][:, 0, :], ob=col("L1_xcond_bp"))
            if layer == 2:
                return dict(n=1, norm=1, mod=False, kw=W["L2_xcond_W_kvc"][:, 0, 0:D],
                            vw=W["L2_xcond_W_kvc"][:, 0, D:2 * D],
                            kb=col("L2_xcond_b_kvc", 0), vb=col("L2_xcond_b_kvc", 1),
                            ow=W["L2_xcond_W_cproj"][:, 0, :], ob=col("L2_xcond_b_cproj"))
            return dict(n=2, norm=None, mod=False, kw=W["L3_xcond_ca_kw"][:, 0, :], vw=W["L3_xcond_ca_vw"][:, 0, :],
                        kb=col("L3_xcond_ca_kb"), vb=col("L3_xcond_ca_vb"),
                        ow=W["L3_xcond_ca_ow"][:, 0, :], ob=col("L3_xcond_ca_ob"))

        CROSS_Q = {
            1: (W["L1_xcond_Wq"][:, 0, :], col("L1_xcond_bq"), A[4], "L1_xq"),
            2: (W["L2_xcond_W_qc"][:, 0, :], col("L2_xcond_b_qc"), XH, None),
            3: (W["L3_xcond_ca_qw"][:, 0, :], col("L3_xcond_ca_qb"), X, "x3_self"),
        }
        SELF = {
            2: (0, [W["L2_xcond_W_qkv"][:, 0, k * D:(k + 1) * D] for k in range(3)],
                [col("L2_xcond_b_qkv", k) for k in range(3)],
                W["L2_xcond_W_proj"][:, 0, :], col("L2_xcond_b_proj")),
            3: (1, [W[f"L3_xcond_sa_{k}w"][:, 0, :] for k in "qkv"],
                [col(f"L3_xcond_sa_{k}b") for k in "qkv"],
                W["L3_xcond_sa_ow"][:, 0, :], col("L3_xcond_sa_ob")),
        }
        FFN = {
            2: ("L2_xcond_W_mlp1", "L2_xcond_b_mlp1", "L2_xcond_W_mlp2", "L2_xcond_b_mlp2", ACT.Gelu_apprx_tanh),
            3: ("L3_xcond_ffn_w1", "L3_xcond_ffn_b1", "L3_xcond_ffn_w2", "L3_xcond_ffn_b2", ACT.Gelu),
        }
        QSCALE = float(DH) ** -0.5
        LNS = [("x_in", 0), ("x0", 0), ("x1", 1), ("x2_self", 1), ("x2_cross", 1), ("x2", 0), ("x3_cross", 0)]

        @block.sync
        def _(sp):
            sp.dma_start(xrows[:, :, :], x.rearrange("b t d -> (b t) d").rearrange("(k p) d -> p k d", p=PW))\
              .then_inc(sem("x_loaded"), 16)
            sp.dma_start(cond_sb[:, :], cond).then_inc(sem("cond_loaded"), 16)
            for name in VECTORS:
                n = place[name]
                v = w[name]
                if len(v.shape) == 2:
                    v = v.rearrange("e n -> (e n)")
                k = v.shape[0] // 128
                sp.dma_start(vrows[n:n + k, :], v.rearrange("(k p) -> k p", p=128)).then_inc(sem("vec_loaded"), 16)
            sp.dma_start(router_b[:, :], w["L0_xcond_router_b"].rearrange("(o e) -> o e", o=1).to_broadcast([128, E]))\
              .then_inc(sem("vec_loaded"), 16)

            for layer in range(layers):
                n0 = B * (layer - 1)

                def load(batch):
                    b, i, p = batch
                    if layer == 0 or (layer == 1 and isinstance(b, int) and b < 2):
                        ge(sp, "ev_ready", B * layer + b - 1)
                        ge(sp, "bn_done", B * layer + b - 1)
                    else:
                        ge(sp, "cxT_ready", NT * (n0 + b - 1))
                    sp.dma_start(cx[:, p, :, :], ctx[bass.ds(b, 1)].rearrange("o (p c) d -> (o p) c d", p=KC))\
                      .then_inc(sem(f"cx_loaded{p}"), 16)

                if layer == 0:
                    load((0, 0, 0))
                    load((1, 0, 1))
                    with sp.Fori(1, B // 2) as i:
                        for p in range(2):
                            load((2 * i + p, i, p))
                    continue

                ge(sp, "q_split", layer)
                for p in range(2):
                    ge(sp, f"q_loaded{p}", 16 * (B // 2) * (layer - 1))
                    ge(sp, f"q_mx_loaded{p}", 16 * (B // 2) * (layer - 1))
                for g in range(NG):
                    for c, src in enumerate((qh_all, ql_all, qh_all)):
                        sp.dma_start(q_all[32 * c:32 * c + 32, g, :, :],
                                     src[32 * g:32 * g + 32, :, :, :].rearrange("p b h t -> p b (h t)"))\
                          .then_inc(sem("q_stacked"), 16)
                sp.wait_ge(sem("q_stacked"), 16 * 3 * NG * layer)

                def q_for(batch, dst, name):
                    b, i, p = batch
                    sp.dma_start(dst[0:96, p, :, :], q_all[:, :, bass.ds(b, 1), :].rearrange("p g o n -> p g (o n)"))\
                      .then_inc(sem(f"{name}{p}"), 16)

                def q_scores(batch):
                    ge(sp, "scores_ready", C * (n0 + batch[0] - 1))
                    q_for(batch, q_st, "q_loaded")

                def q_max(batch):
                    ge(sp, "max_ready", UNITS * (n0 + batch[0] - 1))
                    q_for(batch, q_mx, "q_mx_loaded")

                def stack(batch, piece):
                    b, i, p = batch
                    n = n0 + b
                    lo, hi = PIECES[piece]
                    ge(sp, "v_ready", NT * n + (1, NT)[piece])
                    for g in range(NG):
                        for c, src in enumerate((k_hi, k_hi, k_lo)):
                            sp.dma_start(k_st[32 * c:32 * c + 32, p, g, lo:hi], src[32 * g:32 * g + 32, lo:hi])\
                              .then_inc(sem(f"k_stacked{piece}"), 16)

                def first():
                    q_max((0, 0, 0))
                    q_scores((0, 0, 0))
                    q_max((1, 0, 1))
                    stack((0, 0, 0), 0)
                    load((2, 1, 0))
                    stack((0, 0, 0), 1)
                    stack((1, 0, 1), 0)
                    load((3, 1, 1))

                def attend(batch, following, behind, third):
                    b, i, p = batch
                    if following:
                        stack(following, 1)
                        q_scores(following)
                    if behind:
                        q_max(behind)
                        stack(behind, 0)
                        if not (isinstance(b, int) and b + 4 >= B):
                            load((b + 4, i + 2, p))

                load((0, 0, 0))
                load((1, 0, 1))
                pipeline(sp, first, attend)

            sp.wait_ge(sem("rows_out"), 2)
            sp.dma_start(out.rearrange("b t d -> (b t) d").rearrange("(k p) d -> p k d", p=PW), xrows[:, :, :])\
              .then_inc(sem("stored"), 16)
            sp.wait_ge(sem("stored"), 16)

        @block.gpsimd
        def _(pool):
            pool.memset(ident[:, :], 0.0).then_inc(sem("ident_zero"), 1)
            pool.memset(mean_w[:, :], 1.0 / D).then_inc(sem("consts"), 1)
            pool.memset(ones32[:, :], 1.0).then_inc(sem("consts"), 1)
            pool.memset(eps[:, 0:1], 1e-5).then_inc(sem("consts"), 1)
            pool.memset(eps[:, 1:2], 1e-6).then_inc(sem("consts"), 1)
            pool.memset(sel_mask[:, :, :, :], 1.0).then_inc(sem("consts"), 1)
            pool.wait_ge(sem("ident_zero"), 1)
            pool.affine_select(out=ident[:, :], in_=ident[:, :], compare_op=ALU.not_equal, fill=1.0,
                               base=0, pattern=[[-1, 128]], channel_multiplier=1).then_inc(sem("ident_done"), 1)

            def qk_copy(batch):
                b, i, p = batch
                if not (isinstance(b, int) and b < 2):
                    pool.wait_ge(sem("s0_ready"), b - 1)
                pool.tensor_copy(qk_b[:, p, :], rows_of(A[5], b)).then_inc(sem("qk_copied"), 1)

            ge(pool, "qk_done")
            qk_copy((0, 0, 0))
            qk_copy((1, 0, 1))
            with pool.Fori(1, B // 2) as i:
                for p in range(2):
                    qk_copy((2 * i + p, i, p))

            def self_copies(layer):
                s = SELF[layer][0]

                def copies(batch):
                    b, i, p = batch
                    ge(pool, "ss_ready", B * s + b - 1)
                    pool.tensor_copy(xn_b[:, p, :], rows_of(A[4], b)).then_inc(sem("self_copied"), 1)
                    pool.tensor_copy(kk_b[:, p, :], rows_of(A[6], b)).then_inc(sem("self_copied"), 1)

                ge(pool, "self_qkv", s + 1)
                copies((0, 0, 0))
                copies((1, 0, 1))
                with pool.Fori(1, B // 2) as i:
                    for p in range(2):
                        copies((2 * i + p, i, p))

            def cross_copies(layer):
                cr = cross_of(layer)
                n0 = B * cr["n"]

                def copies(batch):
                    b, i, p = batch
                    if cr["norm"] is not None:
                        ge(pool, "cx_normed", n0 + b - 1)
                        pool.tensor_copy(norm_b[:, p, 0, :], mean_all[:, bass.ds(b, 1), :].rearrange("p o c -> p (o c)"))\
                            .then_inc(sem("norm_copied"), 1)
                        pool.tensor_copy(norm_b[:, p, 1, :],
                                         rstd_all[:, cr["norm"], bass.ds(b, 1), :].rearrange("p o c -> p (o c)"))\
                            .then_inc(sem("norm_copied"), 1)
                    if cr["mod"]:
                        ge(pool, "cxT_done", NT * (b - 1))
                        pool.tensor_copy(mod_b[:, p, :], mod[:, KV_SCALE:KV_SHIFT + 1, bass.ds(b, 1)]
                                         .rearrange("p k o -> p (k o)")).then_inc(sem("mod_copied"), 1)

                if cr["norm"] is None:
                    return
                if layer == 1:
                    ge(pool, "rstd_done", 2)
                copies((0, 0, 0))
                copies((1, 0, 1))
                with pool.Fori(1, B // 2) as i:
                    for p in range(2):
                        copies((2 * i + p, i, p))

            if layers > 1:
                cross_copies(1)
            if layers > 2:
                self_copies(2)
                cross_copies(2)
            if layers > 3:
                self_copies(3)

        @block.scalar
        def _(act):
            for name in WEIGHTS:
                act.dma_start(W[name][:, :, :], w[name].rearrange("(k p) n -> p k n", p=128))\
                   .then_inc(sem("w_loaded"), 16)
            for e in range(E):
                act.dma_start(w1[:, e, :, :], w["L0_xcond_e_w1"][e].rearrange("(k p) n -> p k n", p=128))\
                   .then_inc(sem("w_loaded"), 16)
                act.dma_start(w2[:, e, :, :], w["L0_xcond_e_w2"][e].rearrange("(k p) n -> p k n", p=128))\
                   .then_inc(sem("w_loaded"), 16)
            ge(act, "condT_done")
            act.activation(silu_t[:, :], condT[:, :], ACT.Tanh, scale=0.5).then_inc(sem("cond_tanh"), 1)

            def norm_steps(k):
                ge(act, "ln_centred", k + 1)
                act.activation(SQ[:, :], CEN[:, :], ACT.Square).then_inc(sem("ln_squared"), 1)
                ge(act, "ln_var", k + 1)
                act.activation(halves(STD), pair(1), ACT.Sqrt, bias=eps[:, LNS[k][1]:LNS[k][1] + 1])\
                   .then_inc(sem("ln_std"), 1)

            norm_steps(0)
            ge(act, "mod_done", 2)
            ge(act, "ln_done", 1)
            act.activation(A[4][:, :], XH[:, :], ACT.Identity, scale=col("L0_xcond_ln_gamma"),
                           bias=col("L0_xcond_ln_beta")).then_inc(sem("nx_done"), 1)

            def l0_front(batch):
                b, i, p = batch
                for t in range(NT):
                    ge(act, "cxT0_ready", NT * b + t + 1)
                    if t == 0:
                        ge(act, "s0_ready", b)
                    act.activation(cxT[:, TK * t:TK * t + TK], PS[:, 6, 0:TK], ACT.Copy).then_inc(sem("cxT0_done"), 1)
                ge(act, "neg0_done", b + 1)
                if not (isinstance(b, int) and b < 2):
                    act.wait_ge(sem("p0T_ready"), 2 * (b - 1))
                act.activation(p0[:, p, :].rearrange("q (t k) -> q t k", t=NT), PS[0:T, 3 * p:3 * p + 3, 0:TK], ACT.Exp,
                               bias=neg0[:, p:p + 1], accum_out=sum0[:, p:p + 1]).then_inc(sem("p0_done"), 1)

            def l0_back(batch):
                b, i, p = batch
                for u in range(2):
                    ge(act, "p0T_ready", 2 * b + u + 1)
                    if u == 0:
                        ge(act, "ev_ready", b)
                    act.activation(pT0[:, u * 6 * T:(u + 1) * 6 * T], PS[0:KC, 7, 0:6 * T], ACT.Copy)\
                       .then_inc(sem(f"p0T_done{u}"), 1)
                ge(act, "evT_ready", b + 1)
                act.activation(rows_of(A[6], b), PS[:, 7, 0:T], ACT.Copy).then_inc(sem("evT_done"), 1)

            def l0_both(b, n, more):
                l0_front(n)
                l0_back(b)

            batches(act, l0_front, l0_both, l0_back, True)
            ge(act, "stats_done", B)
            for k in range(2):
                if k == 1:
                    ge(act, "rstd_done", 1)
                act.activation(std_all[:, :, :], var_all[:, :, :], ACT.Sqrt, bias=eps[0:KC, k:k + 1])\
                   .then_inc(sem("std_done"), 1)
            for e in range(E):
                ge(act, "router_shifted", e + 1)
                act.activation(A[e][:, :], A[e][:, :], ACT.Exp).then_inc(sem("router_exp"), 1)
            for k in range(2 * E + 1):
                bias = col("L0_xcond_e_b1", k) if k < 2 * E else col("L0_xcond_gate_b1")
                ge(act, "hid_ready", k + 1)
                if k:
                    ge(act, "hid_done", k)
                act.activation(halves(A[7]), pair(1 + k % 2), ACT.Identity, bias=bias).then_inc(sem("hid_z"), 1)
                act.activation(halves(A[8]), pair(1 + k % 2), ACT.Tanh, bias=half[:, k:k + 1], scale=0.5)\
                   .then_inc(sem("hid_tanh"), 1)
            ge(act, "gate_ready")
            act.activation(halves(A[7]), pair(0), ACT.Tanh, bias=half[:, 7:8], scale=0.25).then_inc(sem("gate_tanh"), 1)

            def cross(layer):
                cr = cross_of(layer)
                n0 = B * cr["n"]
                ge(act, "q_stacked", 16 * 3 * NG * layer)

                def misc(batch, k):
                    b, i, p = batch
                    n = n0 + b
                    kind, t = MISC[k]
                    if kind == "T":
                        ge(act, "cxT_ready", NT * n + t + 1)
                        dst = cxT[:, TK * t:TK * t + TK]
                        if cr["mod"]:
                            if t == 0:
                                ge(act, "mod_copied", b + 1)
                            act.activation(dst, PS[:, MISC_BANK, 0:TK], ACT.Identity, scale=mod_b[:, p, 0:1],
                                           bias=mod_b[:, p, 1:2]).then_inc(sem("cxT_done"), 1)
                        else:
                            act.activation(dst, PS[:, MISC_BANK, 0:TK], ACT.Copy).then_inc(sem("cxT_done"), 1)
                    elif kind == "K":
                        ge(act, "k_ready", NT * n + t + 1)
                        ge(act, f"k_stacked{PIECE_OF[t]}", STACKED * n)
                        act.activation(k_hi[:, TK * t:TK * t + TK], PS[:, MISC_BANK, 0:TK], ACT.Identity, bias=cr["kb"])\
                           .then_inc(sem("k_hi_done"), 1)
                    else:
                        ge(act, "v_ready", NT * n + t + 1)
                        act.activation(v_sb[:, p, TC * t:TC * t + TC, :],
                                       PS[0:KC, MISC_BANK, :].rearrange("p (c d) -> p c d", c=TC), ACT.Copy)\
                           .then_inc(sem("v_done"), 1)

                def first():
                    for k in range(len(MISC)):
                        misc((0, 0, 0), k)
                    for k in range(len(MISC) - 1):
                        misc((1, 0, 1), k)

                def attend(batch, following, behind, _):
                    b, i, p = batch
                    for c in range(C):
                        n = C * (n0 + b) + c
                        ge(act, "scores_ready", n + 1)
                        ge(act, "pv_done", n - 2)
                        lo, hi = SC_BANKS[c % 2]
                        act.activation(probs[:, c % 3, :].rearrange("p (u r) -> p u r", u=2), PS[0:KC, lo:hi, 0:HR],
                                       ACT.Exp).then_inc(sem("exp_done"), 1)
                        if c in SLOT_MISC:
                            of_next, k = SLOT_MISC[c]
                            if following if of_next else behind:
                                misc(following if of_next else behind, k)

                pipeline(act, first, attend)

            def self_attention(layer):
                s = SELF[layer][0]

                def front(batch):
                    b, i, p = batch
                    n = B * s + b
                    ge(act, "sv_ready", n + 1)
                    act.activation(vv_b[:, p, :], PS[0:T, 6, 0:D], ACT.Copy).then_inc(sem("sv_done"), 1)
                    ge(act, "ss_shifted", n + 1)
                    act.activation(s_sh[:, p, :, :], s_sh[:, p, :, :], ACT.Exp).then_inc(sem("ss_exp"), 1)

                def back(batch):
                    b, i, p = batch
                    n = B * s + b
                    ge(act, "spT_ready", n + 1)
                    ge(act, "spv_ready", n)
                    act.activation(halves(pT_b), PS[0:T, 4:6, 0:HR], ACT.Copy).then_inc(sem("spT_done"), 1)

                def both(b, n, more):
                    front(n)
                    back(b)

                batches(act, front, both, back, layer == 2)

            def ffn(layer):
                f = FFN[layer]
                for k in range(DFF // D):
                    ge(act, "ffn_hid_ready", (layer - 2) * 4 + k + 1)
                    act.activation(halves(A[5 + k]), pair(k), f[4], bias=col(f[1], k)).then_inc(sem("ffn_hid_done"), 1)

            if layers > 1:
                norm_steps(1)
                cross(1)
            if layers > 2:
                norm_steps(2)
                self_attention(2)
                norm_steps(3)
                cross(2)
                norm_steps(4)
                ffn(2)
            if layers > 3:
                norm_steps(5)
                self_attention(3)
                cross(3)
                norm_steps(6)
                ffn(3)

        @block.tensor
        def _(pe):
            mm = pe.matmul

            def linear(dst, weights, rows, signal):
                for u in range(2):
                    for k, (wt, r) in enumerate(zip(weights, rows)):
                        last = mm(dst[:, u, :], wt, r(u), start=(k == 0), stop=(k == len(rows) - 1))
                last.then_inc(sem(signal), 1)

            def half_of(t):
                return lambda u: halves(t)[:, u, :]

            ge(pe, "ident_done")
            ge(pe, "x_loaded", 16)
            for k in range(RT):
                last = pe.transpose(PS[:, k // 4, (k % 4) * PW:(k % 4) * PW + PW], xrows[:, k, :], ident[0:PW, 0:PW])
            last.then_inc(sem("xT_ready"), 1)
            ge(pe, "vec_loaded", 16 * (len(VECTORS) + 1))
            pe.transpose(PS[:, 5, 0:nv], vrows[:, :], ident[0:nv, 0:nv]).then_inc(sem("vecT_ready"), 1)
            ge(pe, "cond_loaded", 16)
            pe.transpose(PS[:, 6, 0:B], cond_sb[:, :], ident[0:B, 0:B]).then_inc(sem("condT_ready"), 1)
            ge(pe, "w_loaded", 16 * (len(WEIGHTS) + 2 * E))
            pe.transpose(PS[:, 7, 0:D], W["L0_xcond_Wk"][:, 0, :], ident[:, :]).then_inc(sem("wkT_ready"), 1)
            ge(pe, "silu_done")
            k = 0
            ge(pe, "condT_done")
            for name, m in MODS:
                for j in range(m):
                    rhs = condT if name.startswith("L3") else siluT
                    last = mm(PS[:, 6, k * B:(k + 1) * B], W[name][:, 0, j * D:(j + 1) * D], rhs[:, :],
                              start=True, stop=True)
                    k += 1
            last.then_inc(sem("mod_ready"), 1)

            def norm_steps(k):
                ge(pe, LNS[k][0])
                if k == 0:
                    ge(pe, "consts", 5)
                linear(pair(0), [mean_w[:, :]], [half_of(X)], "ln_mean")
                ge(pe, "ln_squared", k + 1)
                linear(pair(1), [mean_w[:, :]], [half_of(SQ)], "ln_var")

            norm_steps(0)
            ge(pe, "nx_done")
            linear(pair(2), [W["L0_xcond_Wq"][:, 0, :]], [half_of(A[4])], "q0_ready")
            ge(pe, "q0_done")
            ge(pe, "wkT_done")
            ge(pe, "mod_done", 2)
            linear(pair(3), [wkT[:, :]], [half_of(A[5])], "qk_ready")
            ge(pe, "qk_done")

            ge(pe, "qk_done")

            def l0_front(batch):
                b, i, p = batch
                ge(pe, f"cx_loaded{p}", 16 * (i + 1))
                for t in range(NT):
                    ge(pe, "cxT0_done", NT * b + t)
                    for c in range(TC):
                        last = pe.transpose(PS[:, 6, c * KC:(c + 1) * KC], cx[:, p, TC * t + c, :], ident[0:KC, 0:KC])
                    last.then_inc(sem("cxT0_ready"), 1)
                ge(pe, "qk_copied", b + 1)
                ge(pe, "cxT0_done", NT * (b + 1))
                if not (isinstance(b, int) and b < 2):
                    pe.wait_ge(sem("p0_done"), b - 1)
                for t in range(NT):
                    last = mm(PS[0:T, 3 * p + t, 0:TK], qk_b[:, p, :], cxT[:, TK * t:TK * t + TK], start=True, stop=True)
                last.then_inc(sem("s0_ready"), 1)

            def l0_back(batch):
                b, i, p = batch
                for u in range(2):
                    if u == 0:
                        ge_ahead(pe, ("p0_done", b + 1), ("evT_done", b))
                    else:
                        ge_ahead(pe, ("p0T_done0", b + 1))
                    for c in range(6):
                        k = 6 * u + c
                        last = pe.transpose(PS[0:KC, 7, c * T:(c + 1) * T], p0[:, p, k * KC:(k + 1) * KC], ident[0:T, 0:T])
                    last.then_inc(sem("p0T_ready"), 1)
                ge(pe, "p0T_done1", b + 1)
                for c in range(C):
                    last = mm(PS[0:T, 7, 0:D], pT0[:, c * T:(c + 1) * T], cx[:, p, c, :], start=(c == 0), stop=(c == C - 1))
                last.then_inc(sem("ev_ready"), 1)
                ge_ahead(pe, ("ev_done", b + 1))
                pe.transpose(PS[:, 7, 0:T], ev_rows[:, :], ident[0:T, 0:T]).then_inc(sem("evT_ready"), 1)

            def l0_both(b, n, more):
                l0_front(n)
                l0_back(b)

            batches(pe, l0_front, l0_both, l0_back, True)
            ge(pe, "evT_done", B)
            linear(pair(0), [W["L0_xcond_Wv"][:, 0, :]], [half_of(A[6])], "evid_ready")
            ge(pe, "evid_done")
            anchor = lambda u: condT[:, u * 8:(u + 1) * 8].unsqueeze(2).to_broadcast([128, B // 2, T])
            comb = [half_of(A[4]), half_of(A[5]), anchor]
            for e in range(E):
                rw = W["L0_xcond_router_W"]
                linear(pair(1 + e), [rw[:, k, e:e + 1].to_broadcast([128, 128]) for k in range(3)], comb, "router_ready")
            for k in range(2 * E + 1):
                if k == 0:
                    ge(pe, "router_logits", 1)
                elif k == 1:
                    ge(pe, "router_logits", 2)
                else:
                    ge(pe, "hid_tanh", k - 1)
                    ge(pe, "hid_z", k - 1)
                if k < 2 * E:
                    wts = [w1[:, k // 2, j, (k % 2) * D:(k % 2 + 1) * D] for j in range(3)]
                else:
                    wts = [W["L0_xcond_gate_w1"][:, j, :] for j in range(3)]
                linear(pair(1 + k % 2), wts, comb, "hid_ready")
                if k >= 2 and k % 2 == 0:
                    e = k // 2 - 1
                    ge(pe, "hid_done", k)
                    ge(pe, "expert_done" if e else "router_logits", e if e else 3)
                    linear(pair(3), [w2[:, e, j, :] for j in range(2)], [half_of(OALL), half_of(A[3])], "expert_ready")
            ge(pe, "hid_done", 2 * E + 1)
            linear(pair(0), [W["L0_xcond_gate_w2"][:, 0, :]], [half_of(OALL)], "gate_ready")
            ge(pe, "expert_done", E)
            linear(pair(3), [W["L0_xcond_out_w"][:, 0, :]], [half_of(A[6])], "delta_ready")

            def cross(layer):
                cr = cross_of(layer)
                n0 = B * cr["n"]
                wq_, _, src, signal = CROSS_Q[layer]
                if signal:
                    ge(pe, signal)
                if layer == 2:
                    ge(pe, "ln_done", 4)
                linear(pair(2), [wq_], [half_of(src)], "cq_ready")
                ge(pe, "cq_done", layer)
                ge(pe, "dve_consts", 2 + HG)

                def misc(batch, k):
                    b, i, p = batch
                    n = n0 + b
                    kind, t = MISC[k]
                    if k == 0:
                        ge(pe, "v_done", NT * n)
                    else:
                        was, wt = MISC[k - 1]
                        if was == "K":
                            ge(pe, "k_hi_done", NT * n + wt + 1)
                            ge(pe, "k_lo_done", NT * n + wt + 1)
                        else:
                            ge(pe, {"T": "cxT_done", "V": "v_done"}[was], NT * n + wt + 1)
                    if kind == "T":
                        if t == 0:
                            if cr["norm"] is None:
                                ge(pe, f"cx_loaded{p}", 16 * (B // 2 * layer + i + 1))
                            else:
                                ge(pe, "cx_normed", n + 1)
                        for c in range(TC):
                            last = pe.transpose(PS[:, MISC_BANK, c * KC:(c + 1) * KC], cx[:, p, TC * t + c, :],
                                                ident[0:KC, 0:KC])
                        last.then_inc(sem("cxT_ready"), 1)
                    elif kind == "K":
                        ge(pe, "cxT_done", NT * n + t + 1)
                        mm(PS[:, MISC_BANK, 0:TK], cr["kw"], cxT[:, TK * t:TK * t + TK], start=True, stop=True)\
                            .then_inc(sem("k_ready"), 1)
                    else:
                        ge(pe, "cxT_done", NT * n + t + 1)
                        for c in range(TC):
                            k0 = (TC * t + c) * KC
                            last = mm(PS[0:KC, MISC_BANK, c * D:(c + 1) * D], cxT[:, k0:k0 + KC], cr["vw"],
                                      start=True, stop=True)
                        last.then_inc(sem("v_ready"), 1)

                def unit(batch, u):
                    b, i, p = batch
                    n = n0 + b
                    t, rb = u // NP, u % NP
                    if u == 0:
                        ge(pe, f"q_mx_loaded{p}", 16 * (B // 2 * cr["n"] + i + 1))
                        ge(pe, "shift_done", n)
                    if rb == 0:
                        ge(pe, f"k_stacked{PIECE_OF[t]}", STACKED * (n + 1))
                    ge(pe, "max_done", UNITS * n + u - 1)
                    mm(PS[0:PW, MX_BANK + u % 2, 0:TK], q_mx[0:96, p, rb // 2, (rb % 2) * PW:(rb % 2) * PW + PW],
                       k_st[0:96, p, rb // 2, TK * t:TK * t + TK], start=True, stop=True).then_inc(sem("max_ready"), 1)

                def shift(batch):
                    b, i, p = batch
                    ge(pe, "split_done", n0 + b + 1)
                    ge(pe, "max_done", UNITS * (n0 + b + 1))
                    for rb in range(NP):
                        last = mm(PS[96:99, MX_BANK + rb // 4, (rb % 4) * PW:(rb % 4) * PW + PW], msplit[:, rb, :],
                                  ident16[0:PW, 0:PW], start=True, stop=True, skip_group_check=True)
                    last.then_inc(sem("shift_ready"), 1)

                def values(batch, c):
                    b, i, p = batch
                    n = C * (n0 + b) + c
                    ge(pe, "exp_done", n + 1)
                    if c % TC == 0:
                        ge(pe, "v_done", NT * (n0 + b) + c // TC + 1)
                    if c == 0:
                        ge(pe, "attn_read", n0 + b)
                    for g in range(NG):
                        mm(PS[32 * g:32 * g + 32, PV_BANK, 0:GW], v_sb[:, p, c, 32 * g:32 * g + 32],
                           probs[:, c % 3, g * GW:(g + 1) * GW], start=(c == 0), stop=(c == C - 1),
                           skip_group_check=True)

                def sums(batch, c):
                    for g in range(NG):
                        last = mm(PS[32 * g:32 * g + 32, PV_BANK, GW:2 * GW], ones32[0:KC, :],
                                  probs[:, c % 3, g * GW:(g + 1) * GW], start=False, stop=(c == C - 1),
                                  skip_group_check=True)
                    last.then_inc(sem("pv_done"), 1)

                def scores(batch, c):
                    b, i, p = batch
                    n = C * (n0 + b) + c
                    ge(pe, "exp_done", n - 1)
                    if c == 0:
                        ge(pe, f"q_loaded{p}", 16 * (B // 2 * cr["n"] + i + 1))
                        ge(pe, "shift_done", n0 + b + 1)
                    lo, _ = SC_BANKS[c % 2]
                    for g in range(NG):
                        last = mm(PS[0:KC, lo + g // 2, (g % 2) * GW:(g % 2) * GW + GW], k_st[0:ROWS, p, g, c * KC:(c + 1) * KC],
                                  q_st[0:ROWS, p, g, :], start=True, stop=True)
                    last.then_inc(sem("scores_ready"), 1)

                def first():
                    for k in range(len(MISC)):
                        misc((0, 0, 0), k)
                    for k in range(len(MISC) - 1):
                        misc((1, 0, 1), k)
                    for u in range(UNITS):
                        unit((0, 0, 0), u)
                    shift((0, 0, 0))

                def attend(batch, following, behind, _):
                    u = 0
                    for c in range(C):
                        scores(batch, c)
                        tiles = list(range(u, u + MAXES[c])) if following else []
                        u += MAXES[c]
                        if tiles:
                            unit(following, tiles.pop(0))
                        if c in SLOT_MISC:
                            of_next, k = SLOT_MISC[c]
                            if following if of_next else behind:
                                misc(following if of_next else behind, k)
                        if c:
                            values(batch, c - 1)
                        if tiles:
                            unit(following, tiles.pop(0))
                        if c:
                            sums(batch, c - 1)
                        for t in tiles:
                            unit(following, t)
                        if following and c == SHIFT_SLOT:
                            shift(following)
                    values(batch, C - 1)
                    sums(batch, C - 1)

                pipeline(pe, first, attend)
                ge(pe, "attn_all", layer)
                linear(pair(0), [cr["ow"]], [half_of(A[5])], "co_ready")

            def self_attention(layer):
                s, wts, _, ow, _ = SELF[layer]
                ge(pe, f"L{layer}_xn")
                for k in range(2):
                    linear(pair(2 + k), [wts[k]], [half_of(A[4])], "self_lin")
                ge(pe, "self_qkv", s + 1)

                def front(batch):
                    b, i, p = batch
                    n = B * s + b
                    ge(pe, "self_copied", 2 * (n + 1))
                    ge(pe, "sv_done", n)
                    mm(PS[0:T, 6, 0:D], xn_b[:, p, :], wts[2], start=True, stop=True).then_inc(sem("sv_ready"), 1)
                    ge(pe, "sq_masked", n + 1)
                    ge(pe, "so_read", n - 1)
                    ge(pe, "ss_shifted", n)
                    for g in range(NG):
                        for k in range(2):
                            last = mm(PS[0:PW, g, k * T:(k + 1) * T],
                                      qm_b[32 * g:32 * g + 32, p, 2 * k:2 * k + 2, :].rearrange("p h t -> p (h t)"),
                                      kk_b[32 * g:32 * g + 32, p, :], start=True, stop=True)
                    last.then_inc(sem("ss_ready"), 1)

                def back(batch):
                    b, i, p = batch
                    n = B * s + b
                    ge_ahead(pe, ("ss_normed", n + 1))
                    for rb in range(NP):
                        last = pe.transpose(PS[0:T, 4 + rb // 4, (rb % 4) * PW:(rb % 4) * PW + PW], s_sh[:, p, rb, :],
                                            ident[0:PW, 0:PW])
                    last.then_inc(sem("spT_ready"), 1)
                    ge_ahead(pe, ("spT_done", n + 1))
                    if isinstance(b, int):
                        ge(pe, "so_read", n)
                    for g in range(NG):
                        last = mm(PS[32 * g:32 * g + 32, 7, 0:GW], vv_b[:, p, 32 * g:32 * g + 32],
                                  pT_b[:, g * GW:(g + 1) * GW], start=True, stop=True)
                    last.then_inc(sem("spv_ready"), 1)

                def both(b, n, more):
                    front(n)
                    back(b)

                batches(pe, front, both, back, layer == 2)
                ge(pe, f"so_all{layer}")
                linear(pair(0), [ow], [half_of(A[5])], "so_ready")

            def ffn(layer):
                f = FFN[layer]
                ge(pe, f"L{layer}_fn")
                for k in range(DFF // D):
                    linear(pair(k), [W[f[0]][:, 0, k * D:(k + 1) * D]], [half_of(A[4])], "ffn_hid_ready")
                ge(pe, "ffn_hid_done", 4 * (layer - 1))
                linear(pair(0), [W[f[2]][:, k, :] for k in range(4)], [half_of(A[5 + k]) for k in range(4)], "ffn_ready")

            if layers > 1:
                norm_steps(1)
                cross(1)
            if layers > 2:
                norm_steps(2)
                self_attention(2)
                norm_steps(3)
                cross(2)
                norm_steps(4)
                ffn(2)
            if layers > 3:
                norm_steps(5)
                self_attention(3)
                cross(3)
                norm_steps(6)
                ffn(3)
            ge(pe, f"x{layers - 1}")
            for k in range(RT):
                last = pe.transpose(PS[0:PW, 4 + k // 4, (k % 4) * D:(k % 4) * D + D], X[:, k * PW:(k + 1) * PW], ident[:, :])
            last.then_inc(sem("rows_ready"), 1)

        @block.vector
        def _(dve):
            chain = [0]

            def then(instruction):
                chain[0] += 1
                instruction.then_inc(sem("dve_chain"), 1)
                dve.wait_ge(sem("dve_chain"), chain[0])

            ge(dve, "xT_ready")
            dve.tensor_copy(halves(X), pair(0)).then_inc(sem("x_in"), 1)
            ge(dve, "ident_done")
            dve.tensor_copy(ident16[:, :], ident[:, :]).then_inc(sem("dve_consts"), 1)
            then(dve.tensor_reduce(mask[:, :], ident[:, :].rearrange("p (g h d) -> p h g d", g=NG, h=HG), AX.XY, ALU.add))
            ge(dve, "consts", 5)
            for h in range(HG):
                dve.tensor_scalar(sel_mask[:, :, h, :], sel_mask[:, :, h, :], mask[:, h:h + 1], None, ALU.mult)\
                   .then_inc(sem("dve_consts"), 1)
            dve.memset(k_st[96:128, :, :, :], 1.0).then_inc(sem("dve_consts"), 1)
            ge(dve, "condT_ready")
            dve.tensor_copy(condT[:, :], PS[:, 6, 0:B]).then_inc(sem("condT_done"), 1)
            ge(dve, "cond_tanh")
            then(dve.scalar_tensor_tensor(out=siluT[:, :], in0=silu_t[:, :], scalar=1.0, in1=condT[:, :],
                                          op0=ALU.add, op1=ALU.mult))
            dve.tensor_scalar(siluT[:, :], siluT[:, :], 0.5, None, ALU.mult).then_inc(sem("silu_done"), 1)
            ge(dve, "wkT_ready")
            dve.tensor_copy(wkT[:, :], PS[:, 7, 0:D]).then_inc(sem("wkT_done"), 1)
            ge(dve, "vecT_ready")
            then(dve.tensor_copy(vec[:, :], PS[:, 5, 0:nv]))
            then(dve.tensor_scalar(half[:, 0:6], vec[:, place["L0_xcond_e_b1"]:place["L0_xcond_e_b1"] + 6], 0.5, None, ALU.mult))
            then(dve.tensor_scalar(half[:, 6:7], col("L0_xcond_gate_b1"), 0.5, None, ALU.mult))
            then(dve.tensor_scalar(half[:, 7:8], col("L0_xcond_gate_b2"), 0.5, None, ALU.mult))
            m0 = place["L1_xcond_bss_q"]
            for k in (Q_SCALE, KV_SCALE, SCALE_A, SCALE_M):
                then(dve.tensor_scalar(vec[:, m0 + k:m0 + k + 1], vec[:, m0 + k:m0 + k + 1], 1.0, None, ALU.add))
            ge(dve, "mod_ready")
            then(dve.tensor_tensor(mod[:, :, :], PS[:, 6, 0:NM * B].rearrange("p (k b) -> p k b", k=NM),
                                   vec[:, m0:m0 + NM].unsqueeze(2).to_broadcast([128, NM, B]), ALU.add))
            for ga, be, ln in ((GAMMA_1, BETA_1, "L3_xcond_ln1"), (GAMMA_2, BETA_2, "L3_xcond_ln2")):
                then(dve.scalar_tensor_tensor(out=mod[:, be, :], in0=mod[:, ga, :], scalar=col(ln + "_b"),
                                              in1=mod[:, be, :], op0=ALU.mult, op1=ALU.add))
                dve.tensor_scalar(mod[:, ga, :], mod[:, ga, :], col(ln + "_g"), None, ALU.mult).then_inc(sem("mod_done"), 1)

            def norm_steps(k):
                ge(dve, "ln_mean", k + 1)
                dve.tensor_tensor(halves(CEN), halves(X), pair(0), ALU.subtract).then_inc(sem("ln_centred"), 1)
                ge(dve, "ln_std", k + 1)
                then(dve.reciprocal(STD[:, :], STD[:, :]))
                dve.tensor_tensor(XH[:, :], CEN[:, :], STD[:, :], ALU.mult).then_inc(sem("ln_done"), 1)

            def modulate(dst, scale, shift, signal, k):
                ge(dve, "ln_done", k + 1)
                then(dve.tensor_tensor(by_batch(dst), by_batch(XH), spread(scale), ALU.mult))
                dve.tensor_tensor(by_batch(dst), by_batch(dst), spread(shift), ALU.add).then_inc(sem(signal), 1)

            norm_steps(0)
            ge(dve, "q0_ready")
            dve.tensor_scalar(halves(A[5]), pair(2), float(D) ** -0.5, None, ALU.mult).then_inc(sem("q0_done"), 1)
            ge(dve, "qk_ready")
            dve.tensor_copy(halves(A[5]), pair(3)).then_inc(sem("qk_done"), 1)

            def l0_front(batch):
                b, i, p = batch
                ge(dve, f"cx_loaded{p}", 16 * (i + 1))
                for c in range(C):
                    last = dve.bn_stats(stats[:, c, :], cx[:, p, c, :])
                last.then_inc(sem("bn_done"), 1)
                ge(dve, "s0_ready", b + 1)
                dve.wait_ge(sem("bn_done"), b + 1)
                dve.tensor_reduce(neg0[:, p:p + 1], PS[0:T, 3 * p:3 * p + 3, 0:TK], AX.XY, ALU.max)\
                   .then_inc(sem("max0"), 1)
                for c in range(C):
                    last = dve.bn_aggr(aggr[:, c, :], stats[:, c, :])
                last.then_inc(sem("aggr_done"), 1)
                dve.wait_ge(sem("max0"), b + 1)
                dve.tensor_scalar(neg0[:, p:p + 1], neg0[:, p:p + 1], -1.0, None, ALU.mult).then_inc(sem("neg0_done"), 1)
                dve.wait_ge(sem("aggr_done"), b + 1)
                dve.tensor_copy(mean_all[:, bass.ds(b, 1), :].rearrange("p o c -> p (o c)"), aggr[:, :, 0])\
                   .then_inc(sem("stats_mean"), 1)
                dve.tensor_copy(var_all[:, bass.ds(b, 1), :].rearrange("p o c -> p (o c)"), aggr[:, :, 1])\
                   .then_inc(sem("stats_done"), 1)

            def l0_back(batch):
                b, i, p = batch
                ge(dve, "p0_done", b + 1)
                dve.reciprocal(rec0[:, p:p + 1], sum0[:, p:p + 1]).then_inc(sem("rec0_done"), 1)
                ge(dve, "ev_ready", b + 1)
                dve.wait_ge(sem("rec0_done"), b + 1)
                if not (isinstance(b, int) and b < 1):
                    dve.wait_ge(sem("evT_ready"), b)
                dve.tensor_scalar(ev_rows[:, :], PS[0:T, 7, 0:D], rec0[:, p:p + 1], None, ALU.mult)\
                   .then_inc(sem("ev_done"), 1)

            def l0_both(b, n, more):
                l0_front(n)
                l0_back(b)

            batches(dve, l0_front, l0_both, l0_back, True)
            for k in range(2):
                ge(dve, "std_done", k + 1)
                dve.reciprocal(rstd_all[:, k, :, :], std_all[:, :, :]).then_inc(sem("rstd_done"), 1)
            ge(dve, "evid_ready")
            dve.tensor_copy(halves(A[5]), pair(0)).then_inc(sem("evid_done"), 1)
            for e in range(E):
                ge(dve, "router_ready", e + 1)
                dve.tensor_scalar(halves(A[e]), pair(1 + e), router_b[:, e:e + 1], None, ALU.add)\
                   .then_inc(sem("router_logits"), 1)
            dve.wait_ge(sem("router_logits"), E)
            ge(dve, "evid_ready")
            then(dve.tensor_tensor(A[3][:, :], A[0][:, :], A[1][:, :], ALU.max))
            then(dve.tensor_tensor(A[3][:, :], A[3][:, :], A[2][:, :], ALU.max))
            for e in range(E):
                dve.tensor_tensor(A[e][:, :], A[e][:, :], A[3][:, :], ALU.subtract).then_inc(sem("router_shifted"), 1)
            ge(dve, "router_exp", E)
            then(dve.tensor_tensor(A[3][:, :], A[0][:, :], A[1][:, :], ALU.add))
            then(dve.tensor_tensor(A[3][:, :], A[3][:, :], A[2][:, :], ALU.add))
            then(dve.reciprocal(A[3][:, :], A[3][:, :]))
            for e in range(E):
                last = dve.tensor_tensor(A[e][:, :], A[e][:, :], A[3][:, :], ALU.mult)
            then(last)
            for k in range(2 * E + 1):
                ge(dve, "hid_tanh", k + 1)
                ge(dve, "hid_z", k + 1)
                if k >= 2 and k % 2 == 0:
                    ge(dve, "expert_ready", k // 2)
                dve.scalar_tensor_tensor(out=(OALL, A[3])[k % 2][:, :], in0=A[8][:, :], scalar=1.0, in1=A[7][:, :],
                                         op0=ALU.add, op1=ALU.mult).then_inc(sem("hid_done"), 1)
                if k >= 2 and k % 2 == 0:
                    e = k // 2 - 1
                    then(dve.tensor_scalar(halves(A[9]), pair(3), 0.5, col("L0_xcond_e_b2", e), ALU.mult, ALU.add)
                         if e else
                         dve.tensor_scalar(halves(A[6]), pair(3), 0.5, col("L0_xcond_e_b2", e), ALU.mult, ALU.add))
                    if e == 0:
                        dve.tensor_tensor(A[6][:, :], A[6][:, :], A[0][:, :], ALU.mult).then_inc(sem("expert_done"), 1)
                    else:
                        then(dve.tensor_tensor(A[9][:, :], A[9][:, :], A[e][:, :], ALU.mult))
                        dve.tensor_tensor(A[6][:, :], A[6][:, :], A[9][:, :], ALU.add).then_inc(sem("expert_done"), 1)
                    dve.wait_ge(sem("expert_done"), e + 1)
            ge(dve, "delta_ready")
            then(dve.tensor_scalar(halves(A[8]), pair(3), col("L0_xcond_out_b"), None, ALU.add))
            ge(dve, "gate_tanh")
            then(dve.scalar_tensor_tensor(out=A[8][:, :], in0=A[7][:, :], scalar=1.0, in1=A[8][:, :],
                                          op0=ALU.add, op1=ALU.mult))
            dve.scalar_tensor_tensor(out=X[:, :], in0=A[8][:, :], scalar=0.5, in1=X[:, :],
                                     op0=ALU.mult, op1=ALU.add).then_inc(sem("x0"), 1)
            dve.wait_ge(sem("x0"), 1)

            def cross(layer):
                cr = cross_of(layer)
                n0 = B * cr["n"]
                _, qb, _, _ = CROSS_Q[layer]
                ge(dve, "cq_ready", layer)
                dve.tensor_scalar(halves(A[7]), pair(2), qb, QSCALE, ALU.add, ALU.mult).then_inc(sem("cq_done"), 1)
                dve.wait_ge(sem("cq_done"), layer)
                ge(dve, "q_stacked", 16 * 3 * NG * (layer - 1))
                for h in range(HG):
                    last = dve.tensor_scalar(qh_all[:, :, h, :], by_batch(A[7]), mask[:, h:h + 1], None, ALU.mult)
                then(last)
                for h in range(HG):
                    last = dve.scalar_tensor_tensor(out=ql_all[:, :, h, :], in0=by_batch(A[7]), scalar=mask[:, h:h + 1],
                                                    in1=qh_all[:, :, h, :], op0=ALU.mult, op1=ALU.subtract)
                last.then_inc(sem("q_split"), 1)

                def normalise(batch, chunks=range(C)):
                    b, i, p = batch
                    if chunks[0] == 0:
                        ge(dve, f"cx_loaded{p}", 16 * (B // 2 * layer + i + 1))
                        ge(dve, "norm_copied", 2 * (n0 + b + 1))
                    for c in chunks:
                        last = dve.tensor_scalar(cx[:, p, c, :], cx[:, p, c, :], norm_b[:, p, 0, c:c + 1],
                                                 norm_b[:, p, 1, c:c + 1], ALU.subtract, ALU.mult)
                    if chunks[-1] == C - 1:
                        last.then_inc(sem("cx_normed"), 1)

                def k_low(batch, k):
                    kind, t = MISC[k]
                    if kind != "K":
                        return
                    b, i, p = batch
                    n = n0 + b
                    ge(dve, "k_hi_done", NT * n + t + 1)
                    ge(dve, f"k_stacked{PIECE_OF[t]}", STACKED * n)
                    cols = slice(TK * t, TK * t + TK)
                    dve.scalar_tensor_tensor(out=k_lo[:, cols], in0=PS[:, MISC_BANK, 0:TK], scalar=cr["kb"],
                                             in1=k_hi[:, cols], op0=ALU.add, op1=ALU.subtract)\
                       .then_inc(sem("k_lo_done"), 1)

                def unit(batch, u):
                    b, i, p = batch
                    t, rb = u // NP, u % NP
                    ge(dve, "max_ready", UNITS * (n0 + b) + u + 1)
                    dve.tensor_reduce(mx[:, rb, t:t + 1], PS[0:PW, MX_BANK + u % 2, 0:TK], AX.X, ALU.max)\
                       .then_inc(sem("max_done"), 1)

                def shift(batch):
                    b, i, p = batch
                    n = n0 + b

                    def step(instruction, k):
                        instruction.then_inc(sem("split_chain"), 1)
                        dve.wait_ge(sem("split_chain"), 4 * n + k)

                    dve.wait_ge(sem("max_done"), UNITS * (n + 1))
                    step(dve.tensor_reduce(mneg[:, :], mx[:, :, :], AX.X, ALU.max), 1)
                    step(dve.tensor_scalar(msplit[:, :, 0], mneg[:, :], -1.0, None, ALU.mult), 2)
                    step(dve.scalar_tensor_tensor(out=mrest[:, 0, :], in0=mneg[:, :], scalar=-1.0, in1=msplit[:, :, 0],
                                                  op0=ALU.mult, op1=ALU.subtract), 3)
                    step(dve.tensor_copy(msplit[:, :, 1], mrest[:, 0, :]), 4)
                    dve.tensor_tensor(msplit[:, :, 2], mrest[:, 0, :], msplit[:, :, 1], ALU.subtract)\
                       .then_inc(sem("split_done"), 1)
                    ge(dve, "shift_ready", n + 1)
                    dve.tensor_copy(q_st[96:99, p, :, :].rearrange("p (u g) n -> p u (g n)", u=2),
                                    PS[96:99, MX_BANK:MX_BANK + 2, 0:HR]).then_inc(sem("shift_done"), 1)

                def finish(batch):
                    b, i, p = batch
                    n = n0 + b
                    ge(dve, "pv_done", C * (n + 1))
                    dve.tensor_tensor(sel[:, :, :, :].rearrange("p a h t -> p (a h t)"), PS[:, PV_BANK, 0:2 * GW],
                                      sel_mask[:, :, :, :].rearrange("p a h t -> p (a h t)"), ALU.mult)\
                       .then_inc(sem("attn_read"), 1)
                    dve.wait_ge(sem("attn_read"), n + 1)
                    dve.tensor_reduce(osum[:, :, :], sel[:, :, :, :].rearrange("p a h t -> p a t h"), AX.X, ALU.add)\
                       .then_inc(sem("osum_done"), 1)
                    dve.wait_ge(sem("osum_done"), n + 1)
                    dve.reciprocal(orec[:, :], osum[:, 1, :]).then_inc(sem("orec_done"), 1)
                    dve.wait_ge(sem("orec_done"), n + 1)
                    dve.tensor_tensor(rows_of(OALL, b), osum[:, 0, :], orec[:, :], ALU.mult).then_inc(sem("attn_out"), 1)

                def first():
                    if cr["norm"] is not None:
                        normalise((0, 0, 0))
                        normalise((1, 0, 1))
                    for b in range(2):
                        for k in range(len(MISC)):
                            k_low((b, 0, b), k)
                    if cr["norm"] is not None:
                        normalise((2, 1, 0))
                    for u in range(UNITS):
                        unit((0, 0, 0), u)
                    shift((0, 0, 0))

                def attend(batch, following, behind, third):
                    b, i, p = batch
                    u = m = 0
                    for c in range(C):
                        if c == 0 and not (isinstance(b, int) and b == 0):
                            finish((b - 1, None, 1 - p))
                        tiles = list(range(u, u + MAXES[c])) if following else []
                        u += MAXES[c]
                        if tiles:
                            unit(following, tiles.pop(0))
                        if c in SLOT_MISC and not SLOT_MISC[c][0] and behind:
                            k_low(behind, SLOT_MISC[c][1])
                        for t in tiles:
                            unit(following, t)
                        if third and cr["norm"] is not None and NORMS[c]:
                            normalise(third, range(m, m + NORMS[c]))
                        m += NORMS[c]
                        if following and c == SHIFT_SLOT:
                            shift(following)
                    if isinstance(b, int) and b == B - 1:
                        finish(batch)

                pipeline(dve, first, attend)
                dve.wait_ge(sem("attn_out"), n0 + B)
                dve.tensor_scalar(A[5][:, :], OALL[:, :], cr["vb"], None, ALU.add).then_inc(sem("attn_all"), 1)
                ge(dve, "co_ready", layer)
                done = {1: "x1", 2: "x2_cross", 3: "x3_cross"}[layer]
                dve.scalar_tensor_tensor(out=halves(X), in0=pair(0), scalar=cr["ob"], in1=halves(X),
                                         op0=ALU.add, op1=ALU.add).then_inc(sem(done), 1)
                dve.wait_ge(sem(done), 1)

            def self_attention(layer):
                s, _, bs, _, ob = SELF[layer]
                ge(dve, "self_lin", 2 * s + 1)
                then(dve.tensor_scalar(halves(A[5]), pair(2), bs[0], QSCALE, ALU.add, ALU.mult))
                ge(dve, "self_lin", 2 * s + 2)
                dve.tensor_scalar(halves(A[6]), pair(3), bs[1], None, ALU.add).then_inc(sem("self_qkv"), 1)

                def front(batch):
                    b, i, p = batch
                    n = B * s + b
                    ge(dve, "ss_ready", n - 1)
                    for h in range(HG):
                        last = dve.tensor_scalar(qm_b[:, p, h, :], rows_of(A[5], b), mask[:, h:h + 1], None, ALU.mult)
                    last.then_inc(sem("sq_masked"), 1)
                    ge(dve, "ss_ready", n + 1)
                    sc = PS[0:PW, 0:4, 0:PW].rearrange("p g (k t) -> p g k t", k=2)
                    dve.tensor_reduce(s_mx[:, :].rearrange("p (g k) -> p g k", k=2), sc, AX.X, ALU.max)\
                       .then_inc(sem("ss_max"), 1)
                    dve.wait_ge(sem("ss_max"), n + 1)
                    ge(dve, "spT_ready", n - 1)
                    for g in range(NG):
                        last = dve.tensor_tensor(s_sh[:, p, 2 * g:2 * g + 2, :],
                                                 PS[0:PW, g, 0:PW].rearrange("p (k t) -> p k t", k=2),
                                                 s_mx[:, 2 * g:2 * g + 2].unsqueeze(2).to_broadcast([PW, 2, T]), ALU.subtract)
                    last.then_inc(sem("ss_shifted"), 1)
                    ge(dve, "ss_exp", n + 1)
                    dve.tensor_reduce(s_sum[:, :], s_sh[:, p, :, :], AX.X, ALU.add).then_inc(sem("ss_sum"), 1)
                    dve.wait_ge(sem("ss_sum"), n + 1)
                    dve.reciprocal(s_rec[:, :], s_sum[:, :]).then_inc(sem("ss_rec"), 1)
                    dve.wait_ge(sem("ss_rec"), n + 1)
                    dve.tensor_tensor(s_sh[:, p, :, :], s_sh[:, p, :, :],
                                      s_rec[:, :].unsqueeze(2).to_broadcast([PW, NP, T]), ALU.mult)\
                       .then_inc(sem("ss_normed"), 1)

                def back(batch):
                    b, i, p = batch
                    n = B * s + b
                    ge(dve, "spv_ready", n + 1)
                    ge(dve, "so_out", n)
                    dve.tensor_tensor(sel[:, 0, :, :].rearrange("p h t -> p (h t)"), PS[:, 7, 0:GW],
                                      sel_mask[:, 0, :, :].rearrange("p h t -> p (h t)"), ALU.mult)\
                       .then_inc(sem("so_read"), 1)
                    dve.wait_ge(sem("so_read"), n + 1)
                    dve.tensor_reduce(rows_of(OALL, b), sel[:, 0, :, :].rearrange("p h t -> p t h"), AX.X, ALU.add)\
                       .then_inc(sem("so_out"), 1)

                def both(b, n, more):
                    front(n)
                    back(b)

                batches(dve, front, both, back, layer == 2)
                dve.wait_ge(sem("so_out"), B * (s + 1))
                dve.tensor_scalar(A[5][:, :], OALL[:, :], bs[2], None, ALU.add).then_inc(sem(f"so_all{layer}"), 1)
                ge(dve, "so_ready", s + 1)
                if layer == 2:
                    then(dve.tensor_scalar(halves(A[7]), pair(0), ob, None, ALU.add))
                    then(dve.tensor_tensor(by_batch(A[7]), by_batch(A[7]), spread(GATE_A), ALU.mult))
                    dve.tensor_tensor(X[:, :], X[:, :], A[7][:, :], ALU.add).then_inc(sem("x2_self"), 1)
                    dve.wait_ge(sem("x2_self"), 1)
                else:
                    dve.scalar_tensor_tensor(out=halves(X), in0=pair(0), scalar=ob, in1=halves(X),
                                             op0=ALU.add, op1=ALU.add).then_inc(sem("x3_self"), 1)
                    dve.wait_ge(sem("x3_self"), 1)

            def ffn(layer):
                f = FFN[layer]
                ge(dve, "ffn_ready", layer - 1)
                if layer == 2:
                    then(dve.tensor_scalar(halves(CEN), pair(0), col(f[3]), None, ALU.add))
                    then(dve.tensor_tensor(by_batch(CEN), by_batch(CEN), spread(GATE_M), ALU.mult))
                    dve.tensor_tensor(X[:, :], X[:, :], CEN[:, :], ALU.add).then_inc(sem("x2"), 1)
                else:
                    dve.scalar_tensor_tensor(out=halves(X), in0=pair(0), scalar=col(f[3]), in1=halves(X),
                                             op0=ALU.add, op1=ALU.add).then_inc(sem("x3"), 1)
                dve.wait_ge(sem(f"x{layer}"), 1)

            if layers > 1:
                norm_steps(1)
                modulate(A[4], Q_SCALE, Q_SHIFT, "L1_xq", 1)
                cross(1)
            if layers > 2:
                norm_steps(2)
                modulate(A[4], SCALE_A, SHIFT_A, "L2_xn", 2)
                self_attention(2)
                norm_steps(3)
                cross(2)
                norm_steps(4)
                modulate(A[4], SCALE_M, SHIFT_M, "L2_fn", 4)
                ffn(2)
            if layers > 3:
                norm_steps(5)
                modulate(A[4], GAMMA_1, BETA_1, "L3_xn", 5)
                self_attention(3)
                cross(3)
                norm_steps(6)
                modulate(A[4], GAMMA_2, BETA_2, "L3_fn", 6)
                ffn(3)
            ge(dve, "rows_ready")
            for k in range(2):
                dve.tensor_copy(xrows[:, 4 * k:4 * k + 4, :], PS[0:PW, 4 + k, :].rearrange("p (c d) -> p c d", c=4))\
                   .then_inc(sem("rows_out"), 1)


def kernel(**inputs):
    import numpy as _np
    import concourse.bacc as _bacc
    from concourse import mybir as _mybir
    from concourse.bass_utils import run_bass_kernel_spmd as _run

    nc = _bacc.Bacc("TRN2", target_bir_lowering=False, num_devices=1)
    arrays, aps = {}, {}
    for name, value in inputs.items():
        a = _np.ascontiguousarray(value)
        arrays[f"in_{name}"] = a
        aps[name] = nc.dram_tensor(f"in_{name}", a.shape, _mybir.dt.from_np(a.dtype), kind="ExternalInput").ap()
    out = nc.dram_tensor("out_x", inputs["x"].shape, _mybir.dt.float32, kind="ExternalOutput").ap()
    build(nc, aps.pop("x"), aps.pop("cond_1024"), aps.pop("ctx_1024"), aps, out)
    r = _run(nc, [arrays], core_ids=[0])
    return r.results[0]["out_x"]
```

```python
from contextlib import ExitStack

import concourse.bass as bass
from concourse import mybir

F32 = mybir.dt.float32
F16 = mybir.dt.float16
ALU = mybir.AluOpType
ACT = mybir.ActivationFunctionType
AX = mybir.AxisListType

B, T, D = 16, 56, 128
S = 1500
C = 12
KC = S // C
NT = 3
TC = C // NT
TK = S // NT
NH, DH = 16, 8
HG = 4
NG = NH // HG
GW = HG * T
PW = 2 * T
NP = NH // 2
R = B * T
HR = R // 2
RT = R // PW
E = 3
DFF = 4 * D
ROWS = 99
UNITS = NP * NT

SC_BANKS = ((0, 2), (2, 4))
MX_BANK = 4
PV_BANK = 6
MISC_BANK = 7

MISC = [("T", 0), ("T", 1), ("T", 2), ("K", 0), ("K", 1), ("K", 2), ("V", 0), ("V", 1), ("V", 2)]
AHEAD = [(0, k) for k in range(9)] + [(1, k) for k in range(8)]
PEELED = 6
DENSE_BANK, SELF_BANK = 0, 5
SLOT_MISC = {0: (True, 8), 1: (False, 0), 2: (False, 1), 3: (False, 2), 4: (False, 3), 6: (False, 4), 7: (False, 5), 8: (False, 6), 10: (False, 7)}
MAXES = [2, 2, 2, 2, 2, 2, 2, 3, 3, 3, 1, 0]
NORMS = [0, 2, 2, 2, 0, 0, 0, 1, 1, 1, 1, 2]
SHIFT_SLOT = 10
PIECES = ((0, TK), (TK, S))
PIECE_OF = (0, 1, 1)
RUNS = [(0, 2, 4), (3, 5, 7), (6, 8, 10), (9, 10, 12), (11, 11, 12)]
ADDS = sum(last > first for first, last, _ in RUNS)
STACKED = 16 * 3 * NG

WEIGHTS = [
    "L0_xcond_Wq", "L0_xcond_Wk", "L0_xcond_Wv", "L0_xcond_gate_w1", "L0_xcond_gate_w2", "L0_xcond_out_w",
    "L0_xcond_router_W",
    "L1_xcond_Wq", "L1_xcond_Wkv", "L1_xcond_Wp", "L1_xcond_Wss_q", "L1_xcond_Wss_kv",
    "L2_xcond_W_mod", "L2_xcond_W_qkv", "L2_xcond_W_proj", "L2_xcond_W_qc", "L2_xcond_W_kvc", "L2_xcond_W_cproj",
    "L2_xcond_W_mlp1", "L2_xcond_W_mlp2",
    "L3_xcond_aff1_w", "L3_xcond_aff2_w", "L3_xcond_sa_qw", "L3_xcond_sa_kw", "L3_xcond_sa_vw", "L3_xcond_sa_ow",
    "L3_xcond_ca_qw", "L3_xcond_ca_kw", "L3_xcond_ca_vw", "L3_xcond_ca_ow", "L3_xcond_ffn_w1", "L3_xcond_ffn_w2",
]
FIRST_WEIGHTS = ["L0_xcond_Wk", "L0_xcond_Wq", "L1_xcond_Wss_q", "L1_xcond_Wss_kv", "L2_xcond_W_mod", "L3_xcond_aff1_w",
                 "L3_xcond_aff2_w"]
VECTORS = [
    "L0_xcond_ln_gamma", "L0_xcond_ln_beta", "L0_xcond_gate_b1", "L0_xcond_gate_b2", "L0_xcond_out_b",
    "L0_xcond_e_b1", "L0_xcond_e_b2",
    "L1_xcond_bq", "L1_xcond_bkv", "L1_xcond_bp",
    "L2_xcond_b_qkv", "L2_xcond_b_proj", "L2_xcond_b_qc", "L2_xcond_b_kvc", "L2_xcond_b_cproj",
    "L2_xcond_b_mlp1", "L2_xcond_b_mlp2",
    "L3_xcond_ln1_g", "L3_xcond_ln1_b", "L3_xcond_ln2_g", "L3_xcond_ln2_b",
    "L3_xcond_sa_qb", "L3_xcond_sa_kb", "L3_xcond_sa_vb", "L3_xcond_sa_ob",
    "L3_xcond_ca_qb", "L3_xcond_ca_kb", "L3_xcond_ca_vb", "L3_xcond_ca_ob", "L3_xcond_ffn_b1", "L3_xcond_ffn_b2",
    "L1_xcond_bss_q", "L1_xcond_bss_kv", "L2_xcond_b_mod", "L3_xcond_aff1_b", "L3_xcond_aff2_b",
]
MODS = [("L1_xcond_Wss_q", 2), ("L1_xcond_Wss_kv", 2), ("L2_xcond_W_mod", 6), ("L3_xcond_aff1_w", 2), ("L3_xcond_aff2_w", 2)]
(Q_SCALE, Q_SHIFT, KV_SCALE, KV_SHIFT, SHIFT_A, SCALE_A, GATE_A, SHIFT_M, SCALE_M, GATE_M,
 GAMMA_1, BETA_1, GAMMA_2, BETA_2) = range(14)
NM = 14


def build(nc, x, cond, ctx, w, out, layers=4):
    with ExitStack() as stack:
        sems = {}

        def sem(name):
            if name not in sems:
                sems[name] = stack.enter_context(nc.semaphore(name))
            return sems[name]

        def sb(name, shape, dt=F32):
            return stack.enter_context(nc.sbuf_tensor(name, shape, dt))

        PS = stack.enter_context(nc.psum_tensor("PS", [128, 8, 512], F32))

        W = {}
        for name in WEIGHTS:
            rows, cols = w[name].shape
            W[name] = sb(name, [128, rows // 128, cols])
        w1 = sb("w1", [128, E, 3, 2 * D])
        w2 = sb("w2", [128, E, 2, D])
        place, nv = {}, 0
        for name in VECTORS:
            place[name] = nv
            n = 1
            for s in w[name].shape:
                n *= s
            nv += n // 128
        assert nv <= 128
        vrows = sb("vrows", [nv, 128])
        vec = sb("vec", [128, nv])
        router_b = sb("router_b", [128, E])

        std8 = sb("std8", [PW, 2, RT // 2])
        rstd8 = sb("rstd8", [PW, 2, RT // 2])

        def col(name, k=0):
            return vec[:, place[name] + k:place[name] + k + 1]

        half = sb("half", [128, 8])
        ident = sb("ident", [128, 128])
        ident16 = sb("ident16", [128, 128], F16)
        mean_w = sb("mean_w", [128, 128])
        ones32 = sb("ones32", [128, 32])
        mask16 = sb("mask16", [128, NH])
        mask = sb("mask", [128, HG])
        sel_mask = sb("sel_mask", [128, 2, HG, T])
        parity = sb("parity", [PW, 2])
        pair_mask = sb("pair_mask", [PW, 2, D])
        eps = sb("eps", [128, 2])
        wkT = sb("wkT", [128, D])
        cond_sb = sb("cond_sb", [B, D])
        condT = sb("condT", [128, B])
        silu_t = sb("silu_t", [128, B])
        siluT = sb("siluT", [128, B])
        mod = sb("mod", [128, NM, B])

        X = sb("X", [128, R])
        A = [sb(f"A{i}", [128, R]) for i in range(10)]
        CEN, SQ, STD, XH = A[0], A[1], A[2], A[3]
        OALL = sb("OALL", [128, R])

        cx = sb("cx", [KC, 2, C, D])
        cxT = sb("cxT", [128, S])
        v_sb = sb("v_sb", [KC, 2, C, D])
        cx0 = [cx[:, 0, :, :], cx[:, 1, :, :], v_sb[:, 0, :, :], v_sb[:, 1, :, :]]
        xrows = cxT[0:PW, 0:RT * D].rearrange("p (k d) -> p k d", k=RT)
        mean_all = sb("mean_all", [KC, B, C])
        var_all = sb("var_all", [KC, B, C])
        std_all = sb("std_all", [KC, B, C])
        rstd_all = sb("rstd_all", [KC, 2, B, C])
        stats = sb("stats", [KC, C, 6])
        aggr = sb("aggr", [KC, C, 2])
        norm_b = sb("norm_b", [KC, 2, 2, C])
        mod_b = sb("mod_b", [128, 2, 2])

        k_hi = sb("k_hi", [128, S], F16)
        k_lo = sb("k_lo", [128, S], F16)
        k_st = sb("k_st", [128, 2, NG, S], F16)
        q_all = sb("q_all", [96, NG, B, GW], F16)
        q_st = sb("q_st", [128, 2, NG, GW], F16)
        q_mx = sb("q_mx", [96, 2, NG, GW], F16)
        mx = sb("mx", [PW, NP, NT])
        mneg = sb("mneg", [PW, NP])
        mrest = sb("mrest", [PW, 2, NP])
        msplit = sb("msplit", [PW, NP, 3], F16)
        sel = sb("sel", [128, 2, HG, T])
        osum = sb("osum", [128, 2, T])
        orec = sb("orec", [128, T])

        run_sum = [t[0:KC, :] for t in A[8:10]]

        q_parts = sb("q_parts", [128, 4 * R])
        probs = q_parts[0:KC, 0:3 * R].rearrange("p (n r) -> p n r", n=3)
        qh_all = q_parts[:, 0:2 * R].bitcast(F16).rearrange("p (b h t) -> p b h t", b=B, h=HG)
        ql_all = q_parts[:, 2 * R:4 * R].bitcast(F16).rearrange("p (b h t) -> p b h t", b=B, h=HG)

        qk_b = sb("qk_b", [128, 2, T])
        p0 = k_st[0:T, :, :, :].rearrange("p a g s -> p a (g s)").bitcast(F32)[:, :, 0:S]
        pT0 = probs[0:KC, 0, 0:C * T]
        ev_rows = sb("ev_rows", [T, D])
        neg0 = sb("neg0", [T, 2])
        sum0 = sb("sum0", [T, 2])
        rec0 = sb("rec0", [T, 2])
        km_b = q_parts[:, 0:2 * R].rearrange("p (a h t) -> p a h t", a=2, h=NH)
        q_b = A[1][:, 0:2 * T].rearrange("p (a t) -> p a t", a=2)
        xn_b = A[1][:, 2 * T:6 * T].rearrange("p (a j t) -> p a j t", a=2, j=2)
        v2_b = A[0][0:PW, 0:4 * D].rearrange("p (a s d) -> p a s d", a=2, s=2)
        s_sh = [t[0:T, :].rearrange("p (h t) -> p h t", h=NH) for t in A[7:9]]
        pT_b = A[9][0:PW, 0:NP * T]
        s_mx = sb("s_mx", [T, NH])

        def ge(eng, name, value=1):
            if not (isinstance(value, int) and value <= 0):
                eng.wait_ge(sem(name), value)

        def batches(eng, first, both, last):
            first((0, 0, 0))
            for b in range(PEELED):
                both((b, b // 2, b % 2), (b + 1, (b + 1) // 2, (b + 1) % 2), AHEAD[3 * b:3 * b + 3])
            with eng.Fori(PEELED // 2, B // 2 - 1) as i:
                both((2 * i, i, 0), (2 * i + 1, i, 1), [])
                both((2 * i + 1, i, 1), (2 * i + 2, i + 1, 0), [])
            both((B - 2, B // 2 - 1, 0), (B - 1, B // 2 - 1, 1), [])
            last((B - 1, B // 2 - 1, 1))

        def ahead(misc, steps, bank):
            for b, k in steps:
                misc((b, 0, b), k, bank)

        def l0_batches(first, both, last, eng):
            first((0, 0, 0, 0))
            for b in range(3):
                both((b, 0, b % 2, b), (b + 1, (b + 1) // 4, (b + 1) % 2, (b + 1) % 4))
            with eng.Fori(1, B // 4) as i:
                for k in range(4):
                    both((4 * i + k - 1, None, (k + 1) % 2, (k - 1) % 4), (4 * i + k, i, k % 2, k))
            last((B - 1, None, 1, 3))

        def pipeline(eng, first, body):
            def at(b, i=None):
                return (b, b // 2, b % 2) if i is None else (2 * i + b, i + b // 2, b % 2)

            first()
            for b in range(2):
                body(*[at(b + k) for k in range(4)])
            with eng.Fori(1, B // 2 - 2) as i:
                for b in range(2):
                    body(*[at(b + k, i) for k in range(4)])
            for b in range(B - 4, B):
                body(*[at(b + k) if b + k < B else None for k in range(4)])

        def ge_ahead(pe, *waits):
            values = [(name, v if isinstance(v, int) else pe.snap(v)) for name, v in waits]
            pe.wait_ge(sem("ident_done"), 1)
            for name, v in values:
                ge(pe, name, v)

        def added(b, k):
            of = [last - first for first, last, _ in RUNS]
            return sum(of) * b + sum(of[:k])

        def before_in_ring(b, c):
            b, c = (b - 1, c + C - 3) if c < 3 else (b, c - 3)
            return b, [k for k, (first, last, _) in enumerate(RUNS) if first <= c <= last][0], c

        def rows_of(t, b):
            return t[:, bass.ds(b * T, T)]

        def pair(k):
            return PS[:, 2 * k:2 * k + 2, 0:HR]

        def halves(t):
            return t.rearrange("p (u r) -> p u r", u=2) if isinstance(t, bass.AP) else t[:, :].rearrange("p (u r) -> p u r", u=2)

        def by_batch(t):
            return t[:, :].rearrange("p (b t) -> p b t", b=B)

        def spread(k):
            return mod[:, k, :].unsqueeze(2).to_broadcast([128, B, T])

        block = stack.enter_context(nc.Block())

        def cross_of(layer):
            if layer == 1:
                return dict(n=0, norm=0, mod=True, kw=W["L1_xcond_Wkv"][:, 0, 0:D], vw=W["L1_xcond_Wkv"][:, 0, D:2 * D],
                            kb=col("L1_xcond_bkv", 0), vb=col("L1_xcond_bkv", 1),
                            ow=W["L1_xcond_Wp"][:, 0, :], ob=col("L1_xcond_bp"))
            if layer == 2:
                return dict(n=1, norm=1, mod=False, kw=W["L2_xcond_W_kvc"][:, 0, 0:D],
                            vw=W["L2_xcond_W_kvc"][:, 0, D:2 * D],
                            kb=col("L2_xcond_b_kvc", 0), vb=col("L2_xcond_b_kvc", 1),
                            ow=W["L2_xcond_W_cproj"][:, 0, :], ob=col("L2_xcond_b_cproj"))
            return dict(n=2, norm=None, mod=False, kw=W["L3_xcond_ca_kw"][:, 0, :], vw=W["L3_xcond_ca_vw"][:, 0, :],
                        kb=col("L3_xcond_ca_kb"), vb=col("L3_xcond_ca_vb"),
                        ow=W["L3_xcond_ca_ow"][:, 0, :], ob=col("L3_xcond_ca_ob"))

        CROSS_Q = {
            1: (W["L1_xcond_Wq"][:, 0, :], col("L1_xcond_bq"), A[4], "L1_xq"),
            2: (W["L2_xcond_W_qc"][:, 0, :], col("L2_xcond_b_qc"), XH, None),
            3: (W["L3_xcond_ca_qw"][:, 0, :], col("L3_xcond_ca_qb"), X, "x3_self"),
        }
        SELF = {
            2: (0, [W["L2_xcond_W_qkv"][:, 0, k * D:(k + 1) * D] for k in range(3)],
                [col("L2_xcond_b_qkv", k) for k in range(3)],
                W["L2_xcond_W_proj"][:, 0, :], col("L2_xcond_b_proj")),
            3: (1, [W[f"L3_xcond_sa_{k}w"][:, 0, :] for k in "qkv"],
                [col(f"L3_xcond_sa_{k}b") for k in "qkv"],
                W["L3_xcond_sa_ow"][:, 0, :], col("L3_xcond_sa_ob")),
        }
        FFN = {
            2: ("L2_xcond_W_mlp1", "L2_xcond_b_mlp1", "L2_xcond_W_mlp2", "L2_xcond_b_mlp2", ACT.Gelu_apprx_tanh),
            3: ("L3_xcond_ffn_w1", "L3_xcond_ffn_b1", "L3_xcond_ffn_w2", "L3_xcond_ffn_b2", ACT.Gelu),
        }
        QSCALE = float(DH) ** -0.5
        LNS = [("x_in", 0), ("x0", 0), ("x1", 1), ("x2_self", 1), ("x2_cross", 1), ("x2", 0), ("x3_cross", 0)]

        def vector_loads(eng, names, signal):
            for name in names:
                v = w[name]
                if len(v.shape) == 2:
                    v = v.rearrange("e n -> (e n)")
                n, k = place[name], v.shape[0] // 128
                eng.dma_start(vrows[n:n + k, :], v.rearrange("(k p) -> k p", p=128)).then_inc(sem(signal), 16)

        @block.sync
        def _(sp):
            sp.dma_start(xrows[:, :, :], x.rearrange("b t d -> (b t) d").rearrange("(k p) d -> p k d", p=PW))\
              .then_inc(sem("x_loaded"), 16)
            sp.dma_start(cond_sb[:, :], cond).then_inc(sem("cond_loaded"), 16)
            vector_loads(sp, VECTORS[0::2], "vec_loaded")
            sp.dma_start(router_b[:, :], w["L0_xcond_router_b"].rearrange("(o e) -> o e", o=1).to_broadcast([128, E]))\
              .then_inc(sem("vec_loaded"), 16)

            for layer in range(layers):
                n0 = B * (layer - 1)

                def load(batch):
                    b, i, p = batch
                    if layer == 1 and isinstance(b, int) and b < 2:
                        ge(sp, "ev_ready", B - 3 + b)
                        ge(sp, "bn_done", B - 3 + b)
                    else:
                        ge(sp, "cxT_ready", NT * (n0 + b - 1))
                    sp.dma_start(cx[:, p, :, :], ctx[bass.ds(b, 1)].rearrange("o (p c) d -> (o p) c d", p=KC))\
                      .then_inc(sem(f"cx_loaded{p}"), 16)

                def load0(b, r):
                    ge(sp, "ev_ready", b - 3)
                    ge(sp, "bn_done", b - 3)
                    sp.dma_start(cx0[r], ctx[bass.ds(b, 1)].rearrange("o (p c) d -> (o p) c d", p=KC))\
                      .then_inc(sem(f"cx0_loaded{r}"), 16)

                if layer == 0:
                    for b in range(4):
                        load0(b, b)
                    for name in WEIGHTS:
                        if name not in FIRST_WEIGHTS:
                            sp.dma_start(W[name][:, :, :], w[name].rearrange("(k p) n -> p k n", p=128))\
                              .then_inc(sem("w_loaded"), 16)
                    for e in range(E):
                        sp.dma_start(w1[:, e, :, :], w["L0_xcond_e_w1"][e].rearrange("(k p) n -> p k n", p=128))\
                          .then_inc(sem("w_loaded"), 16)
                        sp.dma_start(w2[:, e, :, :], w["L0_xcond_e_w2"][e].rearrange("(k p) n -> p k n", p=128))\
                          .then_inc(sem("w_loaded"), 16)
                    with sp.Fori(1, B // 4) as i:
                        for r in range(4):
                            load0(4 * i + r, r)
                    continue

                def stack(batch, piece):
                    b, i, p = batch
                    n = n0 + b
                    lo, hi = PIECES[piece]
                    if piece == 0:
                        sp.wait_ge(sem("k_ready"), NT * n + 2)
                    elif isinstance(b, int) and b < 2:
                        sp.wait_ge(sem("v_ready"), NT * n + 1)
                    else:
                        sp.wait_ge(sem("scores_ready"), C * (n - 1))
                    for g in range(NG):
                        for c, src in enumerate((k_hi, k_hi, k_lo)):
                            sp.dma_start(k_st[32 * c:32 * c + 32, p, g, lo:hi], src[32 * g:32 * g + 32, lo:hi])\
                              .then_inc(sem(f"k_stacked{piece}"), 16)

                load((0, 0, 0))
                load((1, 0, 1))
                stack((0, 0, 0), 0)
                load((2, 1, 0))
                stack((0, 0, 0), 1)
                stack((1, 0, 1), 0)
                load((3, 1, 1))
                stack((1, 0, 1), 1)

                sp.wait_ge(sem("q_split"), layer)
                for p in range(2):
                    ge(sp, f"q_loaded{p}", 16 * (B // 2) * (layer - 1))
                    ge(sp, f"q_mx_loaded{p}", 16 * (B // 2) * (layer - 1))
                def stack_q(lo, hi, signal):
                    for g in range(NG):
                        for c, src in enumerate((qh_all, ql_all, qh_all)):
                            sp.dma_start(q_all[32 * c:32 * c + 32, g, lo:hi, :],
                                         src[32 * g:32 * g + 32, lo:hi, :, :].rearrange("p b h t -> p b (h t)"))\
                              .then_inc(sem(signal), 16)
                    sp.wait_ge(sem(signal), 16 * 3 * NG * layer)

                def q_for(batch, dst, name):
                    b, i, p = batch
                    sp.dma_start(dst[0:96, p, :, :], q_all[:, :, bass.ds(b, 1), :].rearrange("p g o n -> p g (o n)"))\
                      .then_inc(sem(f"{name}{p}"), 16)

                def q_scores(batch):
                    ge(sp, "scores_ready", C * (n0 + batch[0] - 1))
                    q_for(batch, q_st, "q_loaded")

                def q_max(batch):
                    ge(sp, "max_ready", UNITS * (n0 + batch[0] - 1))
                    q_for(batch, q_mx, "q_mx_loaded")

                def first():
                    stack_q(0, 2, "q_first")
                    q_max((0, 0, 0))
                    q_scores((0, 0, 0))
                    q_max((1, 0, 1))
                    stack_q(2, B, "q_stacked")

                def attend(batch, following, behind, third):
                    b, i, p = batch
                    if following:
                        q_scores(following)
                    if behind:
                        q_max(behind)
                        stack(behind, 0)
                        if not (isinstance(b, int) and b + 4 >= B):
                            load((b + 4, i + 2, p))
                        stack(behind, 1)

                pipeline(sp, first, attend)

            sp.wait_ge(sem("rows_out"), 2)
            sp.dma_start(out.rearrange("b t d -> (b t) d").rearrange("(k p) d -> p k d", p=PW), xrows[:, :, :])\
              .then_inc(sem("stored"), 16)
            sp.wait_ge(sem("stored"), 16)

        @block.gpsimd
        def _(pool):
            pool.memset(ident[:, :], 0.0).then_inc(sem("ident_zero"), 1)
            pool.memset(mean_w[:, :], 1.0 / D).then_inc(sem("consts"), 1)
            pool.memset(ones32[:, :], 1.0).then_inc(sem("consts"), 1)
            pool.memset(eps[:, 0:1], 1e-5).then_inc(sem("consts"), 1)
            pool.memset(eps[:, 1:2], 1e-6).then_inc(sem("consts"), 1)
            pool.memset(sel_mask[:, :, :, :], 1.0).then_inc(sem("consts"), 1)
            pool.memset(pair_mask[:, :, :], 0.0).then_inc(sem("consts"), 1)
            pool.wait_ge(sem("ident_zero"), 1)
            pool.affine_select(out=ident[:, :], in_=ident[:, :], compare_op=ALU.not_equal, fill=1.0,
                               base=0, pattern=[[-1, 128]], channel_multiplier=1).then_inc(sem("ident_done"), 1)

            vector_loads(pool, VECTORS[1::2], "vec_loaded_pool")
            pool.wait_ge(sem("ident_done"), 1)
            pool.wait_ge(sem("consts"), 6)
            pool.memset(k_st[96:128, :, :, :], 1.0).then_inc(sem("k_ones"), 1)

            def qk_copy(batch):
                b, i, p = batch
                if not (isinstance(b, int) and b < 2):
                    pool.wait_ge(sem("s0_ready"), b - 1)
                pool.tensor_copy(qk_b[:, p, :], rows_of(A[5], b)).then_inc(sem("qk_copied"), 1)

            pool.wait_ge(sem("k_ones"), 1)
            pool.wait_ge(sem("qk_done"), 1)
            qk_copy((0, 0, 0))
            qk_copy((1, 0, 1))
            with pool.Fori(1, B // 2) as i:
                for p in range(2):
                    qk_copy((2 * i + p, i, p))

            def self_copies(layer):
                s = SELF[layer][0]

                def copies(batch):
                    b, i, p = batch
                    ge(pool, "ss_ready", B * s + b - 1)
                    pool.tensor_copy(q_b[:, p, :], rows_of(A[5], b)).then_inc(sem("self_copied"), 1)
                    pool.tensor_copy(xn_b[:, p, :, :], rows_of(A[4], b).unsqueeze(1).to_broadcast([128, 2, T]))\
                        .then_inc(sem("self_copied"), 1)
                    pool.tensor_tensor(km_b[:, p, :, :], rows_of(A[6], b).unsqueeze(1).to_broadcast([128, NH, T]),
                                       mask16[:, :].unsqueeze(2).to_broadcast([128, NH, T]), ALU.mult)\
                        .then_inc(sem("self_copied"), 1)

                pool.wait_ge(sem("self_qkv"), s + 1)
                ge(pool, "dve_consts", 2 + 2 * HG)
                copies((0, 0, 0))
                copies((1, 0, 1))
                with pool.Fori(1, B // 2) as i:
                    for p in range(2):
                        copies((2 * i + p, i, p))

            def cross_copies(layer, rest):
                cr = cross_of(layer)
                n0 = B * cr["n"]

                def copies(batch):
                    b, i, p = batch
                    if cr["norm"] is not None:
                        ge(pool, "cx_normed", n0 + b - 1)
                        pool.tensor_copy(norm_b[:, p, 0, :], mean_all[:, bass.ds(b, 1), :].rearrange("p o c -> p (o c)"))\
                            .then_inc(sem("norm_copied"), 1)
                        pool.tensor_copy(norm_b[:, p, 1, :],
                                         rstd_all[:, cr["norm"], bass.ds(b, 1), :].rearrange("p o c -> p (o c)"))\
                            .then_inc(sem("norm_copied"), 1)
                    if cr["mod"]:
                        ge(pool, "cxT_done", NT * (b - 1))
                        pool.tensor_copy(mod_b[:, p, :], mod[:, KV_SCALE:KV_SHIFT + 1, bass.ds(b, 1)]
                                         .rearrange("p k o -> p (k o)")).then_inc(sem("mod_copied"), 1)

                if not rest:
                    if layer == 1:
                        pool.wait_ge(sem("rstd_done"), 2)
                    if cr["norm"] is not None:
                        copies((0, 0, 0))
                        copies((1, 0, 1))
                    return

                def attend(batch, following, behind, third):
                    b, i, p = batch
                    if third and cr["norm"] is not None:
                        copies(third)
                    k = 0
                    for first, last, _ in RUNS:
                        if first == last:
                            continue
                        n = ADDS * (n0 + b) + k
                        chunks = C * (n0 + b) + first
                        pool.wait_ge(sem("exp_done"), chunks + 2)
                        ge(pool, "run_read", n - 1)
                        acc = run_sum[k % 2]
                        for c in range(first + 1, last + 1):
                            if c > first + 1:
                                pool.wait_ge(sem("exp_done"), chunks + c - first + 1)
                                ge(pool, "run_added", added(n0 + b, k) + c - first - 1)
                            pool.tensor_tensor(acc, probs[:, first % 3, :] if c == first + 1 else acc, probs[:, c % 3, :],
                                               ALU.add).then_inc(sem("run_added"), 1)
                        k += 1

                def first():
                    if cr["norm"] is not None:
                        copies((2, 1, 0))

                pipeline(pool, first, attend)

            if layers > 1:
                cross_copies(1, False)
                cross_copies(1, True)
            if layers > 2:
                cross_copies(2, False)
                self_copies(2)
                cross_copies(2, True)
            if layers > 3:
                self_copies(3)
                cross_copies(3, True)

        @block.scalar
        def _(act):
            for name in FIRST_WEIGHTS:
                act.dma_start(W[name][:, :, :], w[name].rearrange("(k p) n -> p k n", p=128))\
                   .then_inc(sem("w_first"), 16)

            def norm_steps(k):
                for u in range(2):
                    act.wait_ge(sem("ln_centred"), 2 * k + u + 1)
                    act.activation(halves(SQ)[:, u, :], halves(CEN)[:, u, :], ACT.Square).then_inc(sem("ln_squared"), 1)
                for u in range(2):
                    act.wait_ge(sem("ln_var"), 2 * k + u + 1)
                    act.activation(std8[:, u, :], PS[0:PW, 4 + u, 0:RT // 2], ACT.Sqrt,
                                   bias=eps[0:PW, LNS[k][1]:LNS[k][1] + 1]).then_inc(sem("ln_std"), 1)

            norm_steps(0)
            act.wait_ge(sem("condT_done"), 1)
            act.activation(silu_t[:, :], condT[:, :], ACT.Tanh, scale=0.5).then_inc(sem("cond_tanh"), 1)

            act.wait_ge(sem("mod_done"), 2)
            act.wait_ge(sem("ln_done"), 2)
            act.activation(A[4][:, :], XH[:, :], ACT.Identity, scale=col("L0_xcond_ln_gamma"),
                           bias=col("L0_xcond_ln_beta")).then_inc(sem("nx_done"), 1)

            def copy_ctx(batch, t):
                b, i, p, r = batch
                act.wait_ge(sem("cxT0_ready"), NT * b + t + 1)
                if t == 0:
                    ge(act, "s0_ready", b)
                act.activation(cxT[:, TK * t:TK * t + TK], PS[:, 6, 0:TK], ACT.Copy).then_inc(sem("cxT0_done"), 1)

            def copy_probs(batch, u):
                b, i, p, r = batch
                act.wait_ge(sem("p0T_ready"), 2 * b + u + 1)
                if u == 0:
                    ge(act, "ev_ready", b)
                act.activation(pT0[:, u * 6 * T:(u + 1) * 6 * T], PS[0:KC, 7, 0:6 * T], ACT.Copy)\
                   .then_inc(sem(f"p0T_done{u}"), 1)

            def l0_exp(batch):
                b, i, p, r = batch
                act.wait_ge(sem("neg0_done"), b + 1)
                act.activation(p0[:, p, :].rearrange("q (t k) -> q t k", t=NT), PS[0:T, 3 * p:3 * p + 3, 0:TK], ACT.Exp,
                               bias=neg0[:, p:p + 1], accum_out=sum0[:, p:p + 1]).then_inc(sem("p0_done"), 1)

            def copy_evidence(batch):
                b, i, p, r = batch
                act.wait_ge(sem("evT_ready"), b + 1)
                act.activation(rows_of(A[6], b), PS[:, 3 * p, 0:T], ACT.Copy).then_inc(sem("evT_done"), 1)

            def l0_first(n):
                for t in range(NT):
                    copy_ctx(n, t)
                l0_exp(n)

            def l0_both(b, n):
                copy_ctx(n, 0)
                copy_probs(b, 0)
                copy_ctx(n, 1)
                copy_probs(b, 1)
                copy_ctx(n, 2)
                l0_exp(n)
                copy_evidence(b)

            def l0_last(b):
                copy_probs(b, 0)
                copy_probs(b, 1)
                copy_evidence(b)

            l0_batches(l0_first, l0_both, l0_last, act)
            def preparation(layer):
                cr = cross_of(layer)
                n0 = B * cr["n"]

                def misc(batch, k, bank=MISC_BANK):
                    b, i, p = batch
                    n = n0 + b
                    kind, t = MISC[k]
                    if kind == "T":
                        act.wait_ge(sem("cxT_ready"), NT * n + t + 1)
                        dst = cxT[:, TK * t:TK * t + TK]
                        if cr["mod"]:
                            if t == 0:
                                act.wait_ge(sem("mod_copied"), b + 1)
                            act.activation(dst, PS[:, bank, 0:TK], ACT.Identity, scale=mod_b[:, p, 0:1],
                                           bias=mod_b[:, p, 1:2]).then_inc(sem("cxT_done"), 1)
                        else:
                            act.activation(dst, PS[:, bank, 0:TK], ACT.Copy).then_inc(sem("cxT_done"), 1)
                    elif kind == "K":
                        act.wait_ge(sem("k_ready"), NT * n + t + 1)
                        ge(act, f"k_stacked{PIECE_OF[t]}", STACKED * n)
                        act.activation(k_hi[:, TK * t:TK * t + TK], PS[:, bank, 0:TK], ACT.Identity, bias=cr["kb"])\
                           .then_inc(sem("k_hi_done"), 1)
                    else:
                        act.wait_ge(sem("v_ready"), NT * n + t + 1)
                        act.activation(v_sb[:, p, TC * t:TC * t + TC, :],
                                       PS[0:KC, bank, :].rearrange("p (c d) -> p c d", c=TC), ACT.Copy)\
                           .then_inc(sem("v_done"), 1)

                return misc

            act.wait_ge(sem("stats_done"), B)
            for k in range(2):
                if k == 1:
                    act.wait_ge(sem("rstd_done"), 1)
                act.activation(std_all[:, :, :], var_all[:, :, :], ACT.Sqrt, bias=eps[0:KC, k:k + 1])\
                   .then_inc(sem("std_done"), 1)
            for e in range(E):
                act.wait_ge(sem("router_shifted"), e + 1)
                act.activation(A[e][:, :], A[e][:, :], ACT.Exp).then_inc(sem("router_exp"), 1)
            for k in range(2 * E + 1):
                bias = col("L0_xcond_e_b1", k) if k < 2 * E else col("L0_xcond_gate_b1")
                act.wait_ge(sem("hid_ready"), k + 1)
                if k:
                    ge(act, "hid_done", k)
                act.activation(halves(A[7]), pair(1 + k % 2), ACT.Identity, bias=bias).then_inc(sem("hid_z"), 1)
                act.activation(halves(A[8]), pair(1 + k % 2), ACT.Tanh, bias=half[:, k:k + 1], scale=0.5)\
                   .then_inc(sem("hid_tanh"), 1)
                if layers > 1:
                    ahead(preparation(1), AHEAD[3 * k:3 * k + 3], DENSE_BANK)
            act.wait_ge(sem("gate_ready"), 1)
            act.activation(halves(A[7]), pair(0), ACT.Tanh, bias=half[:, 7:8], scale=0.25).then_inc(sem("gate_tanh"), 1)

            def cross(layer):
                cr = cross_of(layer)
                n0 = B * cr["n"]
                misc = preparation(layer)
                act.wait_ge(sem("cq_done"), layer)
                ge(act, "q_first", 16 * 3 * NG * (layer - 1))
                ge(act, "q_stacked", 16 * 3 * NG * (layer - 1))
                ge(act, "dve_consts", 2 + 2 * HG)
                for h in range(HG):
                    act.activation(qh_all[:, :, h, :], by_batch(A[7]), ACT.Copy, scale=mask[:, h:h + 1])\
                       .then_inc(sem("q_high"), 1)
                act.wait_ge(sem("q_first"), 16 * 3 * NG * layer)
                act.wait_ge(sem("q_stacked"), 16 * 3 * NG * layer)

                def attend(batch, following, behind, _):
                    b, i, p = batch
                    for c in range(C):
                        n = C * (n0 + b) + c
                        act.wait_ge(sem("scores_ready"), n + 1)
                        ge(act, "pv_done", n - 2)
                        was, k, chunk = before_in_ring(n0 + b, c)
                        if RUNS[k][0] == RUNS[k][1]:
                            act.wait_ge(sem("sums_done"), was + 1)
                        else:
                            ge(act, "run_added", added(was, k) + max(chunk - RUNS[k][0], 1))
                        lo, hi = SC_BANKS[c % 2]
                        act.activation(probs[:, c % 3, :].rearrange("p (u r) -> p u r", u=2), PS[0:KC, lo:hi, 0:HR],
                                       ACT.Exp).then_inc(sem("exp_done"), 1)
                        if c in SLOT_MISC:
                            of_next, k = SLOT_MISC[c]
                            if following if of_next else behind:
                                misc(following if of_next else behind, k)

                pipeline(act, lambda: None, attend)

            def self_attention(layer):
                s = SELF[layer][0]

                misc = preparation(layer)

                def exponentials(batch):
                    b, i, p = batch
                    n = B * s + b
                    act.wait_ge(sem("ss_shifted"), n + 1)
                    act.activation(s_sh[p], s_sh[p], ACT.Exp).then_inc(sem("ss_exp"), 1)

                def back(batch):
                    b, i, p = batch
                    n = B * s + b
                    act.wait_ge(sem("spT_ready"), n + 1)
                    ge(act, "spv_ready", n)
                    act.activation(pT_b, PS[0:PW, 4, 0:NP * T], ACT.Copy).then_inc(sem("spT_done"), 1)

                def both(b, n, beside):
                    ahead(misc, beside[0:1], SELF_BANK)
                    back(b)
                    ahead(misc, beside[1:2], SELF_BANK)
                    exponentials(n)
                    ahead(misc, beside[2:3], SELF_BANK)

                batches(act, exponentials, both, back)

            def ffn(layer):
                f = FFN[layer]
                for k in range(DFF // D):
                    act.wait_ge(sem("ffn_hid_ready"), (layer - 2) * 4 + k + 1)
                    act.activation(halves(A[5 + k]), pair(k), f[4], bias=col(f[1], k)).then_inc(sem("ffn_hid_done"), 1)

            if layers > 1:
                norm_steps(1)
                cross(1)
            if layers > 2:
                norm_steps(2)
                self_attention(2)
                norm_steps(3)
                cross(2)
                norm_steps(4)
                ffn(2)
            if layers > 3:
                norm_steps(5)
                self_attention(3)
                cross(3)
                norm_steps(6)
                ffn(3)

        @block.tensor
        def _(pe):
            mm = pe.matmul

            def linear(dst, weights, rows, signal):
                for u in range(2):
                    for k, (wt, r) in enumerate(zip(weights, rows)):
                        last = mm(dst[:, u, :], wt, r(u), start=(k == 0), stop=(k == len(rows) - 1))
                last.then_inc(sem(signal), 1)

            def half_of(t):
                return lambda u: halves(t)[:, u, :]

            pe.wait_ge(sem("ident_done"), 1)
            pe.wait_ge(sem("x_loaded"), 16)
            for k in range(RT):
                last = pe.transpose(PS[:, k // 4, (k % 4) * PW:(k % 4) * PW + PW], xrows[:, k, :], ident[0:PW, 0:PW])
            last.then_inc(sem("xT_ready"), 1)

            def norm_steps(k):
                ge(pe, LNS[k][0])
                if k == 0:
                    pe.wait_ge(sem("consts"), 6)
                for u in range(2):
                    mm(pair(0)[:, u, :], mean_w[:, :], halves(X)[:, u, :], start=True, stop=True).then_inc(sem("ln_mean"), 1)
                for u in range(2):
                    pe.wait_ge(sem("ln_squared"), 2 * k + u + 1)
                    for j in range(RT // 2):
                        r = (RT // 2 * u + j) * PW
                        last = mm(PS[0:PW, 4 + u, j:j + 1], SQ[:, r:r + PW], mean_w[:, 0:1], start=True, stop=True)
                    last.then_inc(sem("ln_var"), 1)
                for u in range(2):
                    pe.wait_ge(sem("ln_rstd"), 2 * k + u + 1)
                    for j in range(RT // 2):
                        last = mm(PS[:, 2 + u, j * PW:(j + 1) * PW], rstd8[:, u, j:j + 1].to_broadcast([PW, 128]),
                                  ident[0:PW, 0:PW], start=True, stop=True)
                    last.then_inc(sem("ln_spread"), 1)

            norm_steps(0)
            pe.wait_ge(sem("vec_loaded"), 16 * (len(VECTORS[0::2]) + 1))
            pe.wait_ge(sem("vec_loaded_pool"), 16 * len(VECTORS[1::2]))
            pe.transpose(PS[:, 5, 0:nv], vrows[:, :], ident[0:nv, 0:nv]).then_inc(sem("vecT_ready"), 1)
            pe.wait_ge(sem("cond_loaded"), 16)
            pe.transpose(PS[:, 6, 0:B], cond_sb[:, :], ident[0:B, 0:B]).then_inc(sem("condT_ready"), 1)
            pe.wait_ge(sem("w_first"), 16 * len(FIRST_WEIGHTS))
            pe.transpose(PS[:, 7, 0:D], W["L0_xcond_Wk"][:, 0, :], ident[:, :]).then_inc(sem("wkT_ready"), 1)
            pe.wait_ge(sem("silu_done"), 1)
            pe.wait_ge(sem("condT_done"), 1)
            k = 0
            for name, m in MODS:
                for j in range(m):
                    rhs = condT if name.startswith("L3") else siluT
                    last = mm(PS[:, 6, k * B:(k + 1) * B], W[name][:, 0, j * D:(j + 1) * D], rhs[:, :],
                              start=True, stop=True)
                    k += 1
            last.then_inc(sem("mod_ready"), 1)

            pe.wait_ge(sem("nx_done"), 1)
            linear(pair(2), [W["L0_xcond_Wq"][:, 0, :]], [half_of(A[4])], "q0_ready")
            pe.wait_ge(sem("q0_done"), 1)
            pe.wait_ge(sem("wkT_done"), 1)
            pe.wait_ge(sem("mod_done"), 2)
            linear(pair(3), [wkT[:, :]], [half_of(A[5])], "qk_ready")
            pe.wait_ge(sem("qk_done"), 1)

            def turn_ctx(batch, t):
                b, i, p, r = batch
                if t == 0:
                    pe.wait_ge(sem(f"cx0_loaded{r}"), 16 * (i + 1))
                ge(pe, "cxT0_done", NT * b + t)
                for c in range(TC):
                    last = pe.transpose(PS[:, 6, c * KC:(c + 1) * KC], cx0[r][:, TC * t + c, :], ident[0:KC, 0:KC])
                last.then_inc(sem("cxT0_ready"), 1)

            def l0_scores(batch):
                b, i, p, r = batch
                pe.wait_ge(sem("qk_copied"), b + 1)
                pe.wait_ge(sem("cxT0_done"), NT * (b + 1))
                for t in range(NT):
                    last = mm(PS[0:T, 3 * p + t, 0:TK], qk_b[:, p, :], cxT[:, TK * t:TK * t + TK], start=True, stop=True)
                last.then_inc(sem("s0_ready"), 1)

            def turn_probs(batch, u):
                b, i, p, r = batch
                if u == 0:
                    ge_ahead(pe, ("p0_done", b + 1))
                else:
                    ge_ahead(pe, ("p0T_done0", b + 1))
                for c in range(6):
                    k = 6 * u + c
                    last = pe.transpose(PS[0:KC, 7, c * T:(c + 1) * T], p0[:, p, k * KC:(k + 1) * KC], ident[0:T, 0:T])
                last.then_inc(sem("p0T_ready"), 1)

            def l0_evidence(batch):
                b, i, p, r = batch
                pe.wait_ge(sem("p0T_done1"), b + 1)
                for c in range(C):
                    last = mm(PS[0:T, 7, 0:D], pT0[:, c * T:(c + 1) * T], cx0[r][:, c, :], start=(c == 0), stop=(c == C - 1))
                last.then_inc(sem("ev_ready"), 1)
                ge_ahead(pe, ("ev_done", b + 1))
                pe.transpose(PS[:, 3 * p, 0:T], ev_rows[:, :], ident[0:T, 0:T]).then_inc(sem("evT_ready"), 1)

            def l0_first(n):
                for t in range(NT):
                    turn_ctx(n, t)
                l0_scores(n)

            def l0_both(b, n):
                turn_ctx(n, 0)
                turn_probs(b, 0)
                turn_ctx(n, 1)
                turn_probs(b, 1)
                turn_ctx(n, 2)
                ge(pe, "evT_done", b[0])
                l0_scores(n)
                l0_evidence(b)

            def l0_last(b):
                turn_probs(b, 0)
                turn_probs(b, 1)
                ge(pe, "evT_done", b[0])
                l0_evidence(b)

            def preparation(layer):
                cr = cross_of(layer)
                n0 = B * cr["n"]

                def misc(batch, k, bank=MISC_BANK):
                    b, i, p = batch
                    n = n0 + b
                    kind, t = MISC[k]
                    if k == 0:
                        ge(pe, "v_done", NT * n)
                    else:
                        was, wt = MISC[k - 1]
                        if was == "K":
                            pe.wait_ge(sem("k_hi_done"), NT * n + wt + 1)
                            pe.wait_ge(sem("k_lo_done"), NT * n + wt + 1)
                        else:
                            ge(pe, {"T": "cxT_done", "V": "v_done"}[was], NT * n + wt + 1)
                    if kind == "T":
                        if t == 0:
                            if cr["norm"] is None:
                                pe.wait_ge(sem(f"cx_loaded{p}"), 16 * (B // 2 * cr["n"] + i + 1))
                            else:
                                pe.wait_ge(sem("cx_normed"), n + 1)
                        for c in range(TC):
                            last = pe.transpose(PS[:, bank, c * KC:(c + 1) * KC], cx[:, p, TC * t + c, :],
                                                ident[0:KC, 0:KC])
                        last.then_inc(sem("cxT_ready"), 1)
                    elif kind == "K":
                        pe.wait_ge(sem("cxT_done"), NT * n + t + 1)
                        mm(PS[:, bank, 0:TK], cr["kw"], cxT[:, TK * t:TK * t + TK], start=True, stop=True)\
                            .then_inc(sem("k_ready"), 1)
                    else:
                        pe.wait_ge(sem("cxT_done"), NT * n + t + 1)
                        for c in range(TC):
                            k0 = (TC * t + c) * KC
                            last = mm(PS[0:KC, bank, c * D:(c + 1) * D], cxT[:, k0:k0 + KC], cr["vw"],
                                      start=True, stop=True)
                        last.then_inc(sem("v_ready"), 1)

                return misc

            l0_batches(l0_first, l0_both, l0_last, pe)
            pe.wait_ge(sem("w_loaded"), 16 * (len(WEIGHTS) - len(FIRST_WEIGHTS) + 2 * E))
            pe.wait_ge(sem("evT_done"), B)
            linear(pair(0), [W["L0_xcond_Wv"][:, 0, :]], [half_of(A[6])], "evid_ready")
            pe.wait_ge(sem("evid_done"), 1)
            anchor = lambda u: condT[:, u * 8:(u + 1) * 8].unsqueeze(2).to_broadcast([128, B // 2, T])
            comb = [half_of(A[4]), half_of(A[5]), anchor]
            for e in range(E):
                rw = W["L0_xcond_router_W"]
                linear(pair(1 + e), [rw[:, k, e:e + 1].to_broadcast([128, 128]) for k in range(3)], comb, "router_ready")
            for k in range(2 * E + 1):
                if k == 0:
                    pe.wait_ge(sem("router_logits"), 1)
                elif k == 1:
                    pe.wait_ge(sem("router_logits"), 2)
                else:
                    ge(pe, "hid_tanh", k - 1)
                    ge(pe, "hid_z", k - 1)
                if k < 2 * E:
                    wts = [w1[:, k // 2, j, (k % 2) * D:(k % 2 + 1) * D] for j in range(3)]
                else:
                    wts = [W["L0_xcond_gate_w1"][:, j, :] for j in range(3)]
                linear(pair(1 + k % 2), wts, comb, "hid_ready")
                if k >= 2 and k % 2 == 0:
                    e = k // 2 - 1
                    ge(pe, "hid_done", k)
                    ge(pe, "expert_done" if e else "router_logits", e if e else 3)
                    linear(pair(3), [w2[:, e, j, :] for j in range(2)], [half_of(OALL), half_of(A[3])], "expert_ready")
                if layers > 1:
                    ahead(preparation(1), AHEAD[3 * k:3 * k + 3], DENSE_BANK)
            pe.wait_ge(sem("hid_done"), 2 * E + 1)
            if layers > 1:
                ge(pe, "v_done", 2 * NT - 1)
            linear(pair(0), [W["L0_xcond_gate_w2"][:, 0, :]], [half_of(OALL)], "gate_ready")
            pe.wait_ge(sem("expert_done"), E)
            linear(pair(3), [W["L0_xcond_out_w"][:, 0, :]], [half_of(A[6])], "delta_ready")

            def cross(layer):
                cr = cross_of(layer)
                n0 = B * cr["n"]
                wq_, _, src, signal = CROSS_Q[layer]
                if signal:
                    ge(pe, signal)
                if layer == 2:
                    pe.wait_ge(sem("ln_done"), 8)
                linear(pair(2), [wq_], [half_of(src)], "cq_ready")
                pe.wait_ge(sem("cq_done"), layer)
                ge(pe, "dve_consts", 2 + 2 * HG)
                pe.wait_ge(sem("k_ones"), 1)

                misc = preparation(layer)

                def unit(batch, u):
                    b, i, p = batch
                    n = n0 + b
                    t, rb = u // NP, u % NP
                    if u == 0:
                        pe.wait_ge(sem(f"q_mx_loaded{p}"), 16 * (B // 2 * cr["n"] + i + 1))
                        ge(pe, "shift_done", n)
                    if rb == 0:
                        pe.wait_ge(sem(f"k_stacked{PIECE_OF[t]}"), STACKED * (n + 1))
                    ge(pe, "max_done", UNITS * n + u - 1)
                    mm(PS[0:PW, MX_BANK + u % 2, 0:TK], q_mx[0:96, p, rb // 2, (rb % 2) * PW:(rb % 2) * PW + PW],
                       k_st[0:96, p, rb // 2, TK * t:TK * t + TK], start=True, stop=True).then_inc(sem("max_ready"), 1)

                def shift(batch):
                    b, i, p = batch
                    pe.wait_ge(sem("split_done"), n0 + b + 1)
                    pe.wait_ge(sem("max_done"), UNITS * (n0 + b + 1))
                    for rb in range(NP):
                        last = mm(PS[96:99, MX_BANK + rb // 4, (rb % 4) * PW:(rb % 4) * PW + PW], msplit[:, rb, :],
                                  ident16[0:PW, 0:PW], start=True, stop=True, skip_group_check=True)
                    last.then_inc(sem("shift_ready"), 1)

                def values(batch, c):
                    b, i, p = batch
                    n = C * (n0 + b) + c
                    pe.wait_ge(sem("exp_done"), n + 1)
                    if c % TC == 0:
                        pe.wait_ge(sem("v_done"), NT * (n0 + b) + c // TC + 1)
                    if c == 0:
                        ge(pe, "attn_read", n0 + b)
                    for g in range(NG):
                        last = mm(PS[32 * g:32 * g + 32, PV_BANK, 0:GW], v_sb[:, p, c, 32 * g:32 * g + 32],
                           probs[:, c % 3, g * GW:(g + 1) * GW], start=(c == 0), stop=(c == C - 1),
                           skip_group_check=True)
                    last.then_inc(sem("pv_done"), 1)

                def sums(batch, k):
                    b, i, p = batch
                    first, c, _ = RUNS[k]
                    if first < c:
                        pe.wait_ge(sem("run_added"), added(n0 + b, k + 1))
                    for g in range(NG):
                        last = mm(PS[32 * g:32 * g + 32, PV_BANK, GW:2 * GW], ones32[0:KC, :],
                                  (run_sum[k % 2] if first < c else probs[:, c % 3, :])[:, g * GW:(g + 1) * GW],
                                  start=False, stop=(c == C - 1), skip_group_check=True)
                    last.then_inc(sem("run_read" if first < c else "sums_done"), 1)

                def scores(batch, c):
                    b, i, p = batch
                    n = C * (n0 + b) + c
                    ge(pe, "exp_done", n - 1)
                    if c == 0:
                        pe.wait_ge(sem(f"q_loaded{p}"), 16 * (B // 2 * cr["n"] + i + 1))
                        pe.wait_ge(sem("shift_done"), n0 + b + 1)
                    lo, _ = SC_BANKS[c % 2]
                    for g in range(NG):
                        last = mm(PS[0:KC, lo + g // 2, (g % 2) * GW:(g % 2) * GW + GW], k_st[0:ROWS, p, g, c * KC:(c + 1) * KC],
                                  q_st[0:ROWS, p, g, :], start=True, stop=True)
                    last.then_inc(sem("scores_ready"), 1)

                def first():
                    for u in range(UNITS):
                        unit((0, 0, 0), u)
                    shift((0, 0, 0))

                def finish(batch):
                    values(batch, C - 1)
                    for k, run in enumerate(RUNS):
                        if run[2] == C:
                            sums(batch, k)

                def attend(batch, following, behind, _):
                    b, i, p = batch
                    u = 0
                    before = None if isinstance(b, int) and b == 0 else (b - 1, None, 1 - p)
                    for c in range(C):
                        scores(batch, c)
                        tiles = list(range(u, u + MAXES[c])) if following else []
                        u += MAXES[c]
                        if tiles:
                            unit(following, tiles.pop(0))
                        if c == 0 and before:
                            finish(before)
                        if c in SLOT_MISC:
                            of_next, k = SLOT_MISC[c]
                            if following if of_next else behind:
                                misc(following if of_next else behind, k)
                        if c:
                            values(batch, c - 1)
                        if tiles:
                            unit(following, tiles.pop(0))
                        for k, run in enumerate(RUNS):
                            if run[2] == c:
                                sums(batch, k)
                        for t in tiles:
                            unit(following, t)
                        if following and c == SHIFT_SLOT:
                            shift(following)
                    if isinstance(b, int) and b == B - 1:
                        finish(batch)

                pipeline(pe, first, attend)
                pe.wait_ge(sem("attn_all"), layer)
                linear(pair(0), [cr["ow"]], [half_of(A[5])], "co_ready")

            def self_attention(layer):
                s, wts, _, ow, _ = SELF[layer]
                misc = preparation(layer)
                pe.wait_ge(sem(f"L{layer}_xn"), 1)
                for k in range(2):
                    linear(pair(2 + k), [wts[k]], [half_of(A[4])], "self_lin")
                pe.wait_ge(sem("self_qkv"), s + 1)

                def front(batch):
                    b, i, p = batch
                    n = B * s + b
                    pe.wait_ge(sem("self_copied"), 3 * (n + 1))
                    ge(pe, "sv_done", n)
                    mm(PS[0:PW, 6, 0:D], xn_b[:, p, :, :].rearrange("p j t -> p (j t)"), wts[2], start=True, stop=True)\
                        .then_inc(sem("sv_ready"), 1)
                    ge(pe, "ss_shifted", n - 1)
                    ge(pe, "so_out", n - 1)
                    for u in range(2):
                        last = mm(PS[0:T, 2 * p + u, 0:HR], q_b[:, p, :],
                                  km_b[:, p, NP * u:NP * u + NP, :].rearrange("p h t -> p (h t)"), start=True, stop=True)
                    last.then_inc(sem("ss_ready"), 1)

                def turn(batch):
                    b, i, p = batch
                    ge_ahead(pe, ("ss_exp", B * s + b + 1))
                    for rb in range(NP):
                        last = pe.transpose(PS[0:PW, 4, rb * T:(rb + 1) * T],
                                            s_sh[p][:, 2 * rb:2 * rb + 2, :].rearrange("p h t -> p (h t)"), ident[0:T, 0:T])
                    last.then_inc(sem("spT_ready"), 1)

                def values(batch):
                    b, i, p = batch
                    ge_ahead(pe, ("spT_done", B * s + b + 1))
                    for k in range(2):
                        for h in range(2):
                            for g in range(NG):
                                wt = (v2_b[:, p, h, :], pair_mask[:, h, :])[k]
                                last = mm(PS[32 * g:32 * g + 32, 7, k * T:(k + 1) * T], wt[:, 32 * g:32 * g + 32],
                                          pT_b[:, (2 * g + h) * T:(2 * g + h + 1) * T], start=(h == 0), stop=(h == 1),
                                          skip_group_check=True)
                    last.then_inc(sem("spv_ready"), 1)

                def both(b, n, beside):
                    front(n)
                    ahead(misc, beside[0:1], SELF_BANK)
                    turn(b)
                    ahead(misc, beside[1:2], SELF_BANK)
                    values(b)
                    ahead(misc, beside[2:3], SELF_BANK)

                def back(b):
                    turn(b)
                    ge(pe, "so_out", B * s + b[0])
                    values(b)

                batches(pe, front, both, back)
                pe.wait_ge(sem(f"so_all{layer}"), 1)
                linear(pair(0), [ow], [half_of(A[5])], "so_ready")

            def ffn(layer):
                f = FFN[layer]
                pe.wait_ge(sem(f"L{layer}_fn"), 1)
                for k in range(DFF // D):
                    linear(pair(k), [W[f[0]][:, 0, k * D:(k + 1) * D]], [half_of(A[4])], "ffn_hid_ready")
                ge(pe, "ffn_hid_done", 4 * (layer - 1))
                linear(pair(0), [W[f[2]][:, k, :] for k in range(4)], [half_of(A[5 + k]) for k in range(4)], "ffn_ready")

            if layers > 1:
                norm_steps(1)
                cross(1)
            if layers > 2:
                norm_steps(2)
                self_attention(2)
                norm_steps(3)
                cross(2)
                norm_steps(4)
                ffn(2)
            if layers > 3:
                norm_steps(5)
                self_attention(3)
                cross(3)
                norm_steps(6)
                ffn(3)
            pe.wait_ge(sem(f"x{layers - 1}"), 1)
            for k in range(RT):
                last = pe.transpose(PS[0:PW, 4 + k // 4, (k % 4) * D:(k % 4) * D + D], X[:, k * PW:(k + 1) * PW], ident[:, :])
            last.then_inc(sem("rows_ready"), 1)

        @block.vector
        def _(dve):
            chain = [0]

            def then(instruction):
                chain[0] += 1
                instruction.then_inc(sem("dve_chain"), 1)
                dve.wait_ge(sem("dve_chain"), chain[0])

            dve.wait_ge(sem("xT_ready"), 1)
            dve.tensor_copy(halves(X), pair(0)).then_inc(sem("x_in"), 1)
            def norm_steps(k, between=(None, None)):
                for u in range(2):
                    dve.wait_ge(sem("ln_mean"), 2 * k + u + 1)
                    dve.tensor_tensor(halves(CEN)[:, u, :], halves(X)[:, u, :], PS[:, u, 0:HR], ALU.subtract)\
                       .then_inc(sem("ln_centred"), 1)
                if between[0]:
                    between[0]()
                for u in range(2):
                    dve.wait_ge(sem("ln_std"), 2 * k + u + 1)
                    dve.reciprocal(rstd8[:, u, :], std8[:, u, :]).then_inc(sem("ln_rstd"), 1)
                if between[1]:
                    between[1]()
                for u in range(2):
                    dve.wait_ge(sem("ln_spread"), 2 * k + u + 1)
                    dve.tensor_tensor(halves(XH)[:, u, :], halves(CEN)[:, u, :], PS[:, 2 + u, 0:HR], ALU.mult)\
                       .then_inc(sem("ln_done"), 1)

            norm_steps(0)
            dve.wait_ge(sem("ident_done"), 1)
            dve.tensor_copy(ident16[:, :], ident[:, :]).then_inc(sem("dve_consts"), 1)
            dve.tensor_reduce(mask16[:, :], ident[:, :].rearrange("p (h d) -> p h d", h=NH), AX.X, ALU.add)\
               .then_inc(sem("dve_consts"), 1)
            then(dve.tensor_reduce(mask[:, :], ident[:, :].rearrange("p (g h d) -> p h g d", g=NG, h=HG), AX.XY, ALU.add))
            dve.wait_ge(sem("consts"), 6)
            then(dve.tensor_reduce(parity[:, :], ident[0:PW, 0:PW].rearrange("p (j k) -> p j k", j=2), AX.X, ALU.add))
            for h in range(HG):
                dve.tensor_copy(pair_mask[:, h // 2, :].rearrange("p (g m d) -> p g m d", g=NG, m=HG)[:, :, h, :],
                                parity[:, h % 2:h % 2 + 1].unsqueeze(2).to_broadcast([PW, NG, DH]))\
                   .then_inc(sem("dve_consts"), 1)
            for h in range(HG):
                dve.tensor_scalar(sel_mask[:, :, h, :], sel_mask[:, :, h, :], mask[:, h:h + 1], None, ALU.mult)\
                   .then_inc(sem("dve_consts"), 1)
            dve.wait_ge(sem("condT_ready"), 1)
            dve.tensor_copy(condT[:, :], PS[:, 6, 0:B]).then_inc(sem("condT_done"), 1)
            dve.wait_ge(sem("cond_tanh"), 1)
            then(dve.scalar_tensor_tensor(out=siluT[:, :], in0=silu_t[:, :], scalar=1.0, in1=condT[:, :],
                                          op0=ALU.add, op1=ALU.mult))
            dve.tensor_scalar(siluT[:, :], siluT[:, :], 0.5, None, ALU.mult).then_inc(sem("silu_done"), 1)
            dve.wait_ge(sem("wkT_ready"), 1)
            dve.tensor_copy(wkT[:, :], PS[:, 7, 0:D]).then_inc(sem("wkT_done"), 1)
            dve.wait_ge(sem("vecT_ready"), 1)
            then(dve.tensor_copy(vec[:, :], PS[:, 5, 0:nv]))
            then(dve.tensor_scalar(half[:, 0:6], vec[:, place["L0_xcond_e_b1"]:place["L0_xcond_e_b1"] + 6], 0.5, None, ALU.mult))
            then(dve.tensor_scalar(half[:, 6:7], col("L0_xcond_gate_b1"), 0.5, None, ALU.mult))
            then(dve.tensor_scalar(half[:, 7:8], col("L0_xcond_gate_b2"), 0.5, None, ALU.mult))
            m0 = place["L1_xcond_bss_q"]
            for k in (Q_SCALE, KV_SCALE, SCALE_A, SCALE_M):
                then(dve.tensor_scalar(vec[:, m0 + k:m0 + k + 1], vec[:, m0 + k:m0 + k + 1], 1.0, None, ALU.add))
            dve.wait_ge(sem("mod_ready"), 1)
            then(dve.tensor_tensor(mod[:, :, :], PS[:, 6, 0:NM * B].rearrange("p (k b) -> p k b", k=NM),
                                   vec[:, m0:m0 + NM].unsqueeze(2).to_broadcast([128, NM, B]), ALU.add))
            for ga, be, ln in ((GAMMA_1, BETA_1, "L3_xcond_ln1"), (GAMMA_2, BETA_2, "L3_xcond_ln2")):
                then(dve.scalar_tensor_tensor(out=mod[:, be, :], in0=mod[:, ga, :], scalar=col(ln + "_b"),
                                              in1=mod[:, be, :], op0=ALU.mult, op1=ALU.add))
                dve.tensor_scalar(mod[:, ga, :], mod[:, ga, :], col(ln + "_g"), None, ALU.mult).then_inc(sem("mod_done"), 1)

            def modulate(dst, scale, shift, signal, k):
                dve.wait_ge(sem("ln_done"), 2 * (k + 1))
                then(dve.tensor_tensor(by_batch(dst), by_batch(XH), spread(scale), ALU.mult))
                dve.tensor_tensor(by_batch(dst), by_batch(dst), spread(shift), ALU.add).then_inc(sem(signal), 1)

            dve.wait_ge(sem("q0_ready"), 1)
            dve.tensor_scalar(halves(A[5]), pair(2), float(D) ** -0.5, None, ALU.mult).then_inc(sem("q0_done"), 1)
            dve.wait_ge(sem("qk_ready"), 1)
            dve.tensor_copy(halves(A[5]), pair(3)).then_inc(sem("qk_done"), 1)

            def row_stats(batch):
                b, i, p, r = batch
                dve.wait_ge(sem(f"cx0_loaded{r}"), 16 * (i + 1))
                for c in range(C):
                    last = dve.bn_stats(stats[:, c, :], cx0[r][:, c, :])
                last.then_inc(sem("bn_done"), 1)

            def l0_max(batch):
                b, i, p, r = batch
                dve.wait_ge(sem("s0_ready"), b + 1)
                dve.tensor_reduce(neg0[:, p:p + 1], PS[0:T, 3 * p:3 * p + 3, 0:TK], AX.XY, ALU.max)\
                   .then_inc(sem("max0"), 1)
                dve.wait_ge(sem("max0"), b + 1)
                dve.tensor_scalar(neg0[:, p:p + 1], neg0[:, p:p + 1], -1.0, None, ALU.mult).then_inc(sem("neg0_done"), 1)

            def join_stats(batch):
                b, i, p, r = batch
                for c in range(C):
                    last = dve.bn_aggr(aggr[:, c, :], stats[:, c, :])
                last.then_inc(sem("aggr_done"), 1)

            def keep_stats(batch):
                b, i, p, r = batch
                dve.wait_ge(sem("aggr_done"), b + 1)
                dve.tensor_copy(mean_all[:, bass.ds(b, 1), :].rearrange("p o c -> p (o c)"), aggr[:, :, 0])\
                   .then_inc(sem("stats_mean"), 1)
                dve.tensor_copy(var_all[:, bass.ds(b, 1), :].rearrange("p o c -> p (o c)"), aggr[:, :, 1])\
                   .then_inc(sem("stats_done"), 1)

            def l0_recip(batch):
                b, i, p, r = batch
                dve.wait_ge(sem("p0_done"), b + 1)
                dve.reciprocal(rec0[:, p:p + 1], sum0[:, p:p + 1]).then_inc(sem("rec0_done"), 1)

            def l0_evidence(batch):
                b, i, p, r = batch
                dve.wait_ge(sem("ev_ready"), b + 1)
                dve.wait_ge(sem("rec0_done"), b + 1)
                if not (isinstance(b, int) and b < 1):
                    dve.wait_ge(sem("evT_ready"), b)
                dve.tensor_scalar(ev_rows[:, :], PS[0:T, 7, 0:D], rec0[:, p:p + 1], None, ALU.mult)\
                   .then_inc(sem("ev_done"), 1)

            def l0_first(n):
                row_stats(n)
                dve.wait_ge(sem("bn_done"), 1)
                l0_max(n)
                join_stats(n)
                keep_stats(n)

            def l0_both(b, n):
                row_stats(n)
                l0_recip(b)
                dve.wait_ge(sem("bn_done"), n[0] + 1)
                l0_max(n)
                l0_evidence(b)
                join_stats(n)
                keep_stats(n)

            def l0_last(b):
                l0_recip(b)
                l0_evidence(b)

            def preparation(layer):
                cr = cross_of(layer)
                n0 = B * cr["n"]

                def normalise(batch, chunks=range(C)):
                    b, i, p = batch
                    if chunks[0] == 0:
                        ge(dve, f"cx_loaded{p}", 16 * (B // 2 * (layer - 1) + i + 1))
                        dve.wait_ge(sem("norm_copied"), 2 * (n0 + b + 1))
                    for c in chunks:
                        last = dve.tensor_scalar(cx[:, p, c, :], cx[:, p, c, :], norm_b[:, p, 0, c:c + 1],
                                                 norm_b[:, p, 1, c:c + 1], ALU.subtract, ALU.mult)
                    if chunks[-1] == C - 1:
                        last.then_inc(sem("cx_normed"), 1)

                def k_low(batch, k, bank=MISC_BANK):
                    kind, t = MISC[k]
                    if kind != "K":
                        return
                    b, i, p = batch
                    n = n0 + b
                    dve.wait_ge(sem("k_hi_done"), NT * n + t + 1)
                    ge(dve, f"k_stacked{PIECE_OF[t]}", STACKED * n)
                    cols = slice(TK * t, TK * t + TK)
                    dve.scalar_tensor_tensor(out=k_lo[:, cols], in0=PS[:, bank, 0:TK], scalar=cr["kb"],
                                             in1=k_hi[:, cols], op0=ALU.add, op1=ALU.subtract)\
                       .then_inc(sem("k_lo_done"), 1)

                return normalise, k_low

            l0_batches(l0_first, l0_both, l0_last, dve)
            for k in range(2):
                dve.wait_ge(sem("std_done"), k + 1)
                dve.reciprocal(rstd_all[:, k, :, :], std_all[:, :, :]).then_inc(sem("rstd_done"), 1)
            dve.wait_ge(sem("evid_ready"), 1)
            dve.tensor_copy(halves(A[5]), pair(0)).then_inc(sem("evid_done"), 1)
            normalise, k_low = preparation(1)
            for e in range(E):
                dve.wait_ge(sem("router_ready"), e + 1)
                dve.tensor_scalar(halves(A[e]), pair(1 + e), router_b[:, e:e + 1], None, ALU.add)\
                   .then_inc(sem("router_logits"), 1)
                if layers > 1 and e < 2:
                    normalise((e, 0, e))
            dve.wait_ge(sem("router_logits"), E)
            dve.wait_ge(sem("evid_ready"), 1)
            then(dve.tensor_tensor(A[3][:, :], A[0][:, :], A[1][:, :], ALU.max))
            then(dve.tensor_tensor(A[3][:, :], A[3][:, :], A[2][:, :], ALU.max))
            for e in range(E):
                dve.tensor_tensor(A[e][:, :], A[e][:, :], A[3][:, :], ALU.subtract).then_inc(sem("router_shifted"), 1)
            dve.wait_ge(sem("router_exp"), E)
            then(dve.tensor_tensor(A[3][:, :], A[0][:, :], A[1][:, :], ALU.add))
            then(dve.tensor_tensor(A[3][:, :], A[3][:, :], A[2][:, :], ALU.add))
            then(dve.reciprocal(A[3][:, :], A[3][:, :]))
            for e in range(E):
                last = dve.tensor_tensor(A[e][:, :], A[e][:, :], A[3][:, :], ALU.mult)
            then(last)
            for k in range(2 * E + 1):
                dve.wait_ge(sem("hid_tanh"), k + 1)
                dve.wait_ge(sem("hid_z"), k + 1)
                if k >= 2 and k % 2 == 0:
                    ge(dve, "expert_ready", k // 2)
                dve.scalar_tensor_tensor(out=(OALL, A[3])[k % 2][:, :], in0=A[8][:, :], scalar=1.0, in1=A[7][:, :],
                                         op0=ALU.add, op1=ALU.mult).then_inc(sem("hid_done"), 1)
                if layers > 1:
                    ahead(k_low, AHEAD[3 * k:3 * k + 3], DENSE_BANK)
                if k >= 2 and k % 2 == 0:
                    e = k // 2 - 1
                    then(dve.tensor_scalar(halves(A[9]), pair(3), 0.5, col("L0_xcond_e_b2", e), ALU.mult, ALU.add)
                         if e else
                         dve.tensor_scalar(halves(A[6]), pair(3), 0.5, col("L0_xcond_e_b2", e), ALU.mult, ALU.add))
                    if e == 0:
                        dve.tensor_tensor(A[6][:, :], A[6][:, :], A[0][:, :], ALU.mult).then_inc(sem("expert_done"), 1)
                    else:
                        then(dve.tensor_tensor(A[9][:, :], A[9][:, :], A[e][:, :], ALU.mult))
                        dve.tensor_tensor(A[6][:, :], A[6][:, :], A[9][:, :], ALU.add).then_inc(sem("expert_done"), 1)
                    dve.wait_ge(sem("expert_done"), e + 1)
            dve.wait_ge(sem("delta_ready"), 1)
            then(dve.tensor_scalar(halves(A[8]), pair(3), col("L0_xcond_out_b"), None, ALU.add))
            dve.wait_ge(sem("gate_tanh"), 1)
            then(dve.scalar_tensor_tensor(out=A[8][:, :], in0=A[7][:, :], scalar=1.0, in1=A[8][:, :],
                                          op0=ALU.add, op1=ALU.mult))
            dve.scalar_tensor_tensor(out=X[:, :], in0=A[8][:, :], scalar=0.5, in1=X[:, :],
                                     op0=ALU.mult, op1=ALU.add).then_inc(sem("x0"), 1)
            dve.wait_ge(sem("x0"), 1)

            def cross(layer):
                cr = cross_of(layer)
                n0 = B * cr["n"]
                _, qb, _, _ = CROSS_Q[layer]
                dve.wait_ge(sem("cq_ready"), layer)
                dve.tensor_scalar(halves(A[7]), pair(2), qb, QSCALE, ALU.add, ALU.mult).then_inc(sem("cq_done"), 1)
                dve.wait_ge(sem("cq_done"), layer)
                ge(dve, "q_first", 16 * 3 * NG * (layer - 1))
                ge(dve, "q_stacked", 16 * 3 * NG * (layer - 1))
                for h in range(HG):
                    ge(dve, "q_high", HG * (layer - 1) + h + 1)
                    last = dve.scalar_tensor_tensor(out=ql_all[:, :, h, :], in0=by_batch(A[7]), scalar=mask[:, h:h + 1],
                                                    in1=qh_all[:, :, h, :], op0=ALU.mult, op1=ALU.subtract)
                last.then_inc(sem("q_split"), 1)

                normalise, k_low = preparation(layer)

                def unit(batch, u):
                    b, i, p = batch
                    t, rb = u // NP, u % NP
                    dve.wait_ge(sem("max_ready"), UNITS * (n0 + b) + u + 1)
                    dve.tensor_reduce(mx[:, rb, t:t + 1], PS[0:PW, MX_BANK + u % 2, 0:TK], AX.X, ALU.max)\
                       .then_inc(sem("max_done"), 1)

                def shift(batch):
                    b, i, p = batch
                    n = n0 + b

                    def step(instruction, k):
                        instruction.then_inc(sem("split_chain"), 1)
                        dve.wait_ge(sem("split_chain"), 4 * n + k)

                    dve.wait_ge(sem("max_done"), UNITS * (n + 1))
                    step(dve.tensor_reduce(mneg[:, :], mx[:, :, :], AX.X, ALU.max), 1)
                    step(dve.tensor_scalar(msplit[:, :, 0], mneg[:, :], -1.0, None, ALU.mult), 2)
                    step(dve.scalar_tensor_tensor(out=mrest[:, 0, :], in0=mneg[:, :], scalar=-1.0, in1=msplit[:, :, 0],
                                                  op0=ALU.mult, op1=ALU.subtract), 3)
                    step(dve.tensor_copy(msplit[:, :, 1], mrest[:, 0, :]), 4)
                    dve.tensor_tensor(msplit[:, :, 2], mrest[:, 0, :], msplit[:, :, 1], ALU.subtract)\
                       .then_inc(sem("split_done"), 1)
                    dve.wait_ge(sem("shift_ready"), n + 1)
                    dve.tensor_copy(q_st[96:99, p, :, :].rearrange("p (u g) n -> p u (g n)", u=2),
                                    PS[96:99, MX_BANK:MX_BANK + 2, 0:HR]).then_inc(sem("shift_done"), 1)

                def finish(batch):
                    b, i, p = batch
                    n = n0 + b
                    dve.wait_ge(sem("sums_done"), n + 1)
                    dve.tensor_tensor(sel[:, :, :, :].rearrange("p a h t -> p (a h t)"), PS[:, PV_BANK, 0:2 * GW],
                                      sel_mask[:, :, :, :].rearrange("p a h t -> p (a h t)"), ALU.mult)\
                       .then_inc(sem("attn_read"), 1)
                    dve.wait_ge(sem("attn_read"), n + 1)
                    dve.tensor_reduce(osum[:, :, :], sel[:, :, :, :].rearrange("p a h t -> p a t h"), AX.X, ALU.add)\
                       .then_inc(sem("osum_done"), 1)
                    dve.wait_ge(sem("osum_done"), n + 1)
                    dve.reciprocal(orec[:, :], osum[:, 1, :]).then_inc(sem("orec_done"), 1)
                    dve.wait_ge(sem("orec_done"), n + 1)
                    dve.tensor_tensor(rows_of(OALL, b), osum[:, 0, :], orec[:, :], ALU.mult).then_inc(sem("attn_out"), 1)

                def first():
                    if cr["norm"] is not None:
                        normalise((2, 1, 0))
                    for u in range(UNITS):
                        unit((0, 0, 0), u)
                    shift((0, 0, 0))

                def attend(batch, following, behind, third):
                    b, i, p = batch
                    u = m = 0
                    for c in range(C):
                        tiles = list(range(u, u + MAXES[c])) if following else []
                        u += MAXES[c]
                        if tiles:
                            unit(following, tiles.pop(0))
                        if c in SLOT_MISC and not SLOT_MISC[c][0] and behind:
                            k_low(behind, SLOT_MISC[c][1])
                        if c == 0 and not (isinstance(b, int) and b == 0):
                            finish((b - 1, None, 1 - p))
                        for t in tiles:
                            unit(following, t)
                        if third and cr["norm"] is not None and NORMS[c]:
                            normalise(third, range(m, m + NORMS[c]))
                        m += NORMS[c]
                        if following and c == SHIFT_SLOT:
                            shift(following)
                    if isinstance(b, int) and b == B - 1:
                        finish(batch)

                pipeline(dve, first, attend)
                dve.wait_ge(sem("attn_out"), n0 + B)
                dve.tensor_scalar(A[5][:, :], OALL[:, :], cr["vb"], None, ALU.add).then_inc(sem("attn_all"), 1)
                dve.wait_ge(sem("co_ready"), layer)
                done = {1: "x1", 2: "x2_cross", 3: "x3_cross"}[layer]
                dve.scalar_tensor_tensor(out=halves(X), in0=pair(0), scalar=cr["ob"], in1=halves(X),
                                         op0=ALU.add, op1=ALU.add).then_inc(sem(done), 1)
                dve.wait_ge(sem(done), 1)

            def self_attention(layer):
                s, _, bs, _, ob = SELF[layer]
                normalise, k_low = preparation(layer)
                dve.wait_ge(sem("self_lin"), 2 * s + 1)
                then(dve.tensor_scalar(halves(A[5]), pair(2), bs[0], QSCALE, ALU.add, ALU.mult))
                dve.wait_ge(sem("self_lin"), 2 * s + 2)
                dve.tensor_scalar(halves(A[6]), pair(3), bs[1], None, ALU.add).then_inc(sem("self_qkv"), 1)

                def front(batch):
                    b, i, p = batch
                    n = B * s + b
                    dve.wait_ge(sem("sv_ready"), n + 1)
                    dve.tensor_tensor(v2_b[:, p, :, :], PS[0:PW, 6, 0:D].unsqueeze(1).to_broadcast([PW, 2, D]),
                                      pair_mask[:, :, :], ALU.mult).then_inc(sem("sv_done"), 1)
                    dve.wait_ge(sem("ss_ready"), n + 1)
                    sc = PS[0:T, 2 * p:2 * p + 2, 0:HR].rearrange("p u (h t) -> p u h t", h=NP)
                    ge(dve, "ss_shifted", n)
                    mx_u = s_mx[:, :].rearrange("p (u h) -> p u h", u=2)
                    dve.tensor_reduce(mx_u, sc, AX.X, ALU.max).then_inc(sem("ss_max"), 1)
                    ge(dve, "spT_ready", n - 1)
                    dve.wait_ge(sem("ss_max"), n + 1)
                    dve.tensor_tensor(s_sh[p].rearrange("p (u h) t -> p u h t", u=2), sc,
                                      mx_u.unsqueeze(3).to_broadcast([T, 2, NP, T]), ALU.subtract)\
                       .then_inc(sem("ss_shifted"), 1)

                def back(batch):
                    b, i, p = batch
                    n = B * s + b
                    dve.wait_ge(sem("spv_ready"), n + 1)
                    dve.reciprocal(orec[:, :], PS[:, 7, T:2 * T]).then_inc(sem("so_rec"), 1)
                    dve.wait_ge(sem("so_rec"), n + 1)
                    dve.tensor_tensor(rows_of(OALL, b), PS[:, 7, 0:T], orec[:, :], ALU.mult).then_inc(sem("so_out"), 1)

                def both(b, n, beside):
                    front(n)
                    ahead(k_low, beside[0:2], SELF_BANK)
                    back(b)
                    ahead(k_low, beside[2:3], SELF_BANK)

                batches(dve, front, both, back)
                dve.wait_ge(sem("so_out"), B * (s + 1))
                dve.tensor_scalar(A[5][:, :], OALL[:, :], bs[2], None, ALU.add).then_inc(sem(f"so_all{layer}"), 1)
                dve.wait_ge(sem("so_ready"), s + 1)
                if layer == 2:
                    then(dve.tensor_scalar(halves(A[7]), pair(0), ob, None, ALU.add))
                    then(dve.tensor_tensor(by_batch(A[7]), by_batch(A[7]), spread(GATE_A), ALU.mult))
                    dve.tensor_tensor(X[:, :], X[:, :], A[7][:, :], ALU.add).then_inc(sem("x2_self"), 1)
                    dve.wait_ge(sem("x2_self"), 1)
                else:
                    dve.scalar_tensor_tensor(out=halves(X), in0=pair(0), scalar=ob, in1=halves(X),
                                             op0=ALU.add, op1=ALU.add).then_inc(sem("x3_self"), 1)
                    dve.wait_ge(sem("x3_self"), 1)

            def ffn(layer):
                f = FFN[layer]
                ge(dve, "ffn_ready", layer - 1)
                if layer == 2:
                    then(dve.tensor_scalar(halves(CEN), pair(0), col(f[3]), None, ALU.add))
                    then(dve.tensor_tensor(by_batch(CEN), by_batch(CEN), spread(GATE_M), ALU.mult))
                    dve.tensor_tensor(X[:, :], X[:, :], CEN[:, :], ALU.add).then_inc(sem("x2"), 1)
                else:
                    dve.scalar_tensor_tensor(out=halves(X), in0=pair(0), scalar=col(f[3]), in1=halves(X),
                                             op0=ALU.add, op1=ALU.add).then_inc(sem("x3"), 1)
                dve.wait_ge(sem(f"x{layer}"), 1)

            if layers > 1:
                norm_steps(1)
                modulate(A[4], Q_SCALE, Q_SHIFT, "L1_xq", 1)
                cross(1)
            if layers > 2:
                normalise, _ = preparation(2)
                norm_steps(2, (lambda: normalise((0, 0, 0)), lambda: normalise((1, 0, 1))))
                modulate(A[4], SCALE_A, SHIFT_A, "L2_xn", 2)
                self_attention(2)
                norm_steps(3)
                cross(2)
                norm_steps(4)
                modulate(A[4], SCALE_M, SHIFT_M, "L2_fn", 4)
                ffn(2)
            if layers > 3:
                norm_steps(5)
                modulate(A[4], GAMMA_1, BETA_1, "L3_xn", 5)
                self_attention(3)
                cross(3)
                norm_steps(6)
                modulate(A[4], GAMMA_2, BETA_2, "L3_fn", 6)
                ffn(3)
            dve.wait_ge(sem("rows_ready"), 1)
            for k in range(2):
                dve.tensor_copy(xrows[:, 4 * k:4 * k + 4, :], PS[0:PW, 4 + k, :].rearrange("p (c d) -> p c d", c=4))\
                   .then_inc(sem("rows_out"), 1)


def kernel(**inputs):
    import numpy as _np
    import concourse.bacc as _bacc
    from concourse import mybir as _mybir
    from concourse.bass_utils import run_bass_kernel_spmd as _run

    nc = _bacc.Bacc("TRN2", target_bir_lowering=False, num_devices=1)
    arrays, aps = {}, {}
    for name, value in inputs.items():
        a = _np.ascontiguousarray(value)
        arrays[f"in_{name}"] = a
        aps[name] = nc.dram_tensor(f"in_{name}", a.shape, _mybir.dt.from_np(a.dtype), kind="ExternalInput").ap()
    out = nc.dram_tensor("out_x", inputs["x"].shape, _mybir.dt.float32, kind="ExternalOutput").ap()
    build(nc, aps.pop("x"), aps.pop("cond_1024"), aps.pop("ctx_1024"), aps, out)
    r = _run(nc, [arrays], core_ids=[0])
    return r.results[0]["out_x"]
```
